# Optimizing a Trainium2 kernel written in Bass

```python
import numpy as np
import jax
import jax.numpy as jnp

def _softmax(x, axis=-1):
    return jax.nn.softmax(x, axis=axis)

def _gelu(x):
    return jax.nn.gelu(x, approximate=True)

def _silu(x):
    return jax.nn.silu(x)

def _sigmoid(x):
    return jax.nn.sigmoid(x)

def _layernorm(x, axis=-1, eps=1e-05):
    m = jnp.mean(x, axis=axis, keepdims=True)
    v = jnp.var(x, axis=axis, keepdims=True)
    return (x - m) / jnp.sqrt(v + eps)

def _scatter_add(tgt, idx, src, axis=0):
    return tgt.at[idx].add(src)

def _segment_sum(src, seg, n):
    return jax.ops.segment_sum(src, seg, n)
kernel_name = 'mk_seq_postln_d1_jaxref_r4_957358'

def setup_inputs(seed: int=0):
    np.random.seed(seed)
    _w = jnp.asarray

    def _L0_attn_setup():
        import jax, jax.numpy as jnp
        import numpy as np
        N_HEAD = 16

        def _rope_cos_sin(T, D):
            half = D // 2
            i = jnp.arange(half, dtype=jnp.float32)
            alpha = 1.0 / 10000.0 ** (2.0 * i / D)
            ang = jnp.arange(T, dtype=jnp.float32)[:, None] * alpha
            return (jnp.cos(ang), jnp.sin(ang))

        def _apply_rope(t, cos, sin):
            half = t.shape[-1] // 2
            xr, xi = (t[..., :half], t[..., half:])
            return jnp.concatenate([xr * cos - xi * sin, xr * sin + xi * cos], axis=-1)
        key = jax.random.key(seed)
        ks = jax.random.split(key, 5)
        B, T, C = (4, 512, 256)
        s = 0.02
        x = jax.random.normal(ks[0], (B, T, C), jnp.float32)
        wq = jax.random.normal(ks[1], (C, C), jnp.float32) * s
        wk = jax.random.normal(ks[2], (C, C), jnp.float32) * s
        wv = jax.random.normal(ks[3], (C, C), jnp.float32) * s
        wp = jax.random.normal(ks[4], (C, C), jnp.float32) * s
        zb = jnp.zeros((C,), jnp.float32)
        return {'x': x, 'wq': wq, 'bq': zb, 'wk': wk, 'bk': zb, 'wv': wv, 'bv': zb, 'wp': wp, 'bp': zb}
    _L0_attn_in = _L0_attn_setup()

    def _L0_ffn_setup():
        import jax, jax.numpy as jnp
        import numpy as np
        TOP_K = 8
        NUM_EXPERTS = 32
        HIDDEN = 256
        EXPERT_DIM = 128
        key = jax.random.key(seed)
        k1, k2, k3, k4 = jax.random.split(key, 4)
        hidden_states = jax.random.normal(k1, (1, 512, HIDDEN), dtype=jnp.float32)
        gate_w = jax.random.normal(k2, (NUM_EXPERTS, HIDDEN), dtype=jnp.float32) * 0.02
        gate_up_w = jax.random.normal(k3, (NUM_EXPERTS, 2 * EXPERT_DIM, HIDDEN), dtype=jnp.float32) * 0.02
        down_w = jax.random.normal(k4, (NUM_EXPERTS, HIDDEN, EXPERT_DIM), dtype=jnp.float32) * 0.02
        return {'hidden_states': hidden_states, 'gate_w': gate_w, 'gate_up_w': gate_up_w, 'down_w': down_w}
    _L0_ffn_in = _L0_ffn_setup()
    _d = {'L0_attn_x': _L0_attn_in['x'], 'L0_attn_wq': _L0_attn_in['wq'], 'L0_attn_bq': _L0_attn_in['bq'], 'L0_attn_wk': _L0_attn_in['wk'], 'L0_attn_bk': _L0_attn_in['bk'], 'L0_attn_wv': _L0_attn_in['wv'], 'L0_attn_bv': _L0_attn_in['bv'], 'L0_attn_wp': _L0_attn_in['wp'], 'L0_attn_bp': _L0_attn_in['bp'], 'L0_ffn_gate_w': _L0_ffn_in['gate_w'], 'L0_ffn_gate_up_w': _L0_ffn_in['gate_up_w'], 'L0_ffn_down_w': _L0_ffn_in['down_w']}
    _x0 = _d['L0_attn_x']
    _d['L0_attn_x'] = jax.random.normal(jax.random.fold_in(jax.random.key(seed), 1), (16, 512, 256), dtype=_x0.dtype)
    del _x0
    return _d

def reference(L0_attn_x, L0_attn_wq, L0_attn_bq, L0_attn_wk, L0_attn_bk, L0_attn_wv, L0_attn_bv, L0_attn_wp, L0_attn_bp, L0_ffn_gate_w, L0_ffn_gate_up_w, L0_ffn_down_w):

    def _L0_attn_ref(x, wq, bq, wk, bk, wv, bv, wp, bp):
        import jax, jax.numpy as jnp
        import numpy as np
        N_HEAD = 16

        def _rope_cos_sin(T, D):
            half = D // 2
            i = jnp.arange(half, dtype=jnp.float32)
            alpha = 1.0 / 10000.0 ** (2.0 * i / D)
            ang = jnp.arange(T, dtype=jnp.float32)[:, None] * alpha
            return (jnp.cos(ang), jnp.sin(ang))

        def _apply_rope(t, cos, sin):
            half = t.shape[-1] // 2
            xr, xi = (t[..., :half], t[..., half:])
            return jnp.concatenate([xr * cos - xi * sin, xr * sin + xi * cos], axis=-1)
        B, T, C = x.shape
        H = N_HEAD
        D = C // H

        def heads(w, b):
            return (x @ w.T + b).reshape(B, T, H, D).transpose(0, 2, 1, 3)
        q, k, v = (heads(wq, bq), heads(wk, bk), heads(wv, bv))
        cos, sin = _rope_cos_sin(T, D)
        q = _apply_rope(q, cos, sin)
        k = _apply_rope(k, cos, sin)
        scale = 1.0 / np.sqrt(D).astype(np.float32)
        att = jnp.einsum('bhtd,bhsd->bhts', q, k) * scale
        causal = jnp.tril(jnp.ones((T, T), bool))
        att = jnp.where(causal, att, jnp.float32(-jnp.inf))
        att = jax.nn.softmax(att, axis=-1)
        y = jnp.einsum('bhts,bhsd->bhtd', att, v)
        y = y.transpose(0, 2, 1, 3).reshape(B, T, C)
        return y @ wp.T + bp

    def _L0_ffn_ref(hidden_states, gate_w, gate_up_w, down_w):
        import jax, jax.numpy as jnp
        import numpy as np
        TOP_K = 8
        NUM_EXPERTS = 32
        HIDDEN = 256
        EXPERT_DIM = 128
        B, S, H = hidden_states.shape
        x = hidden_states.reshape(-1, H)
        logits = x @ gate_w.T
        probs = jax.nn.softmax(logits.astype(jnp.float32), axis=-1)
        top_w, top_idx = jax.lax.top_k(probs, TOP_K)
        top_w = top_w / jnp.sum(top_w, axis=-1, keepdims=True)
        top_w = top_w.astype(x.dtype)
        comb = jnp.sum(jax.nn.one_hot(top_idx, NUM_EXPERTS, dtype=x.dtype) * top_w[..., None], axis=1)

        def body(acc, ws):
            guw, dw, w_e = ws
            gu = x @ guw.T
            g, u = jnp.split(gu, 2, axis=-1)
            y = u * jax.nn.silu(g) @ dw.T
            return (acc + y * w_e[:, None], None)
        init = jnp.zeros_like(x)
        out, _ = jax.lax.scan(body, init, (gate_up_w, down_w, comb.T))
        return out.reshape(B, S, H)
    x = L0_attn_x
    x = _layernorm(x + _L0_attn_ref(x, L0_attn_wq, L0_attn_bq, L0_attn_wk, L0_attn_bk, L0_attn_wv, L0_attn_bv, L0_attn_wp, L0_attn_bp), axis=-1)
    x = _layernorm(x + _L0_ffn_ref(x, L0_ffn_gate_w, L0_ffn_gate_up_w, L0_ffn_down_w), axis=-1)
    return x

_drawn_inputs = setup_inputs


def setup_inputs(seed=0):
    import zlib

    import numpy as np

    out = dict(_drawn_inputs(seed))
    spreads = {'L0_attn_bq': (0.0, 0.8),
     'L0_attn_bk': (0.0, 0.8),
     'L0_attn_bv': (0.0, 0.1),
     'L0_attn_bp': (0.0, 0.1)}
    factors = {'L0_attn_wq': 8.0,
     'L0_attn_wk': 8.0,
     'L0_attn_wv': 4.666,
     'L0_ffn_gate_w': 8.0,
     'L0_ffn_gate_up_w': 8.0,
     'L0_ffn_down_w': 8.0}
    for name, (base, spread) in spreads.items():
        noise = np.random.default_rng([zlib.crc32(name.encode()), seed]).standard_normal(out[name].shape)
        drawn = base * np.exp(spread * noise) if base else spread * noise
        out[name] = jnp.asarray(drawn.astype(out[name].dtype))
    for name, factor in factors.items():
        out[name] = (out[name] * factor).astype(out[name].dtype)
    return out
```

```python
from contextlib import ExitStack

import numpy as np

import concourse.bass as bass
import concourse.mybir as mybir

F32 = mybir.dt.float32
BF16 = mybir.dt.bfloat16
F16 = mybir.dt.float16
ALU = mybir.AluOpType
ACT = mybir.ActivationFunctionType
AX = mybir.AxisListType

P = 128
B, T, C = 16, 512, 256
H, D = 16, 16
E, F, TOPK = 32, 128, 8
NT = T // P
NC = C // P
NQ = H // 4
HALF = D // 2
EPS = 1e-5
NEG = -1e30
KS = 6 * D
KX = KS + 3
OFF = [0, 512, 896, 1152]
TOT = 1280
MUNITS = [(3, 0, 1), (3, 1, 1), (2, 0, 1), (2, 1, 1), (1, 0, 2), (0, 0, 2)]
NM = 2 * len(MUNITS)
PAIRS = E // 2


def build(nc, x, wq, bq, wk, bk, wv, bv, wp, bp, gate_w, gate_up_w, down_w,
          cos_t, sin_t, ident_h, mask_h, out, NB=B):
    parts_dram = nc.dram_tensor("qk_parts", [B, 2, H * KS, T], BF16, kind="Internal").ap()
    att_dram = nc.dram_tensor("attention", [B, H, 2, D, T], F32, kind="Internal").ap()
    x1_dram = nc.dram_tensor("x1_scratch", [B, T, C], F32, kind="Internal").ap()
    mm_dram = nc.dram_tensor("mm_scratch", [E, F], F32, kind="Internal").ap()

    with ExitStack() as ctx:
        def sb(name, shape, dt=F32):
            return ctx.enter_context(nc.sbuf_tensor(name, shape, dt))

        def sem(name):
            return ctx.enter_context(nc.semaphore(name))

        gu_hi = sb("gu_hi", [P, E, NC, 2, F], F16)
        gu_lo = sb("gu_lo", [P, E, NC, 2, F], F16)
        dn_hi = sb("dn_hi", [P, E, C], F16)
        dn_lo = sb("dn_lo", [P, E, C], F16)
        wqT = sb("wqT", [P, NC, C])
        wkT = sb("wkT", [P, NC, C])
        wvT = sb("wvT", [P, NC, C])
        wpT = sb("wpT", [P, NC, C])
        gateT = sb("gateT", [P, NC, E])
        cosT = sb("cosT", [P, T])
        sinT = sb("sinT", [P, T])
        bqc = sb("bqc", [P, 2])
        bkc = sb("bkc", [P, 2])
        bv_b = sb("bv_b", [P, C])
        bp_b = sb("bp_b", [P, C])
        ident = sb("ident", [P, P])
        identb = sb("identb", [P, P], BF16)
        maskq = sb("maskq", [P, P], BF16)
        maskk = sb("maskk", [P, P], BF16)
        mgu = sb("mgu", [P, E, 2])
        mx2 = sb("mx2", [P, 2, 2])
        rcp = sb("rcp", [P, 2, 2])
        rinv = sb("rinv", [P, NC])
        rg4 = sb("rg4", [P, E])
        rc = sb("rc", [P, NC])
        mhalf = sb("mhalf", [P, NT])
        qs = sb("qs", [P, 2, 4, T], BF16)
        ks = sb("ks", [P, 2, 4, T], BF16)
        vx = sb("vx", [P, NT, H, 2 * D])
        work = sb("work", [P, 4 * TOT])
        pT = work[:, :].rearrange("p (r h n) -> p r h n", r=2, h=2)
        xin = sb("xin", [P, NT, C])
        xTden = sb("xTden", [P, NC, T])
        ynum = sb("ynum", [P, NC, T])
        qf = sb("qf", [P, 2, T])
        pbuf = sb("pbuf", [P, 2, 3, T], BF16)
        yev = sb("yev", [P, 2, T])
        gm = yev[:, 0, 0:NC * E].rearrange("p (m e) -> p m e", m=NC)
        mm = yev[:, 1, 0:E]
        mn = sb("mn", [P, 2, NT, 2])
        mr = sb("mr", [P, 2, NT, 2])
        mp = sb("mp", [P, 2, NT, 3, 2], BF16)
        mrow = sb("mrow", [6, 2, T], BF16)
        x1 = sb("x1", [P, NT, C])
        x1Toev = sb("x1Toev", [P, NC, T])
        xh_n = sb("xh_n", [P, NC, T], F16)
        xl_n = sb("xl_n", [P, NC, T], F16)
        xh = sb("xh", [P, NC, T], F16)
        xl = sb("xl", [P, NC, T], F16)
        combT = sb("combT", [3 * E, T], BF16)
        selT = sb("selT", [3 * E, E], BF16)
        ono = sb("ono", [P, NT, C])
        st = sb("st", [P, 2, NT, 6])
        mv = sb("mv", [P, 2, NT, 2])
        ve = sb("ve", [P, 2, NT])
        rs = sb("rs", [P, 2, NT])
        lg = sb("lg", [P, NT, E])
        lg2 = sb("lg2", [P, NT, E])
        v8 = sb("v8", [P, NT, 8])
        msk, le = lg2, lg
        sm = sb("sm", [P, NT])
        cp = sb("cp", [P, NT, 3, E], BF16)
        sg = work[:, 0:2 * T].rearrange("p (r t) -> p r t", r=2)
        hf = work[:, 2 * T:4 * T].rearrange("p (r t) -> p r t", r=2)
        hh = work[:, 4 * T:5 * T].bitcast(F16).rearrange("p (r t) -> p r t", r=2)
        hl = work[:, 5 * T:6 * T].bitcast(F16).rearrange("p (r t) -> p r t", r=2)

        ps = ctx.enter_context(nc.psum_tensor("ps", [P, 8, 512], F32))
        BANK_G, BANK_U, BANK_Y, BANK_S, BANK_PV, BANK_BC = 0, 1, 4, 4, 6, 6
        psf = ps[:, :, :].rearrange("p b n -> p (b n)")

        s_cst = sem("s_cst")
        s_wnat = sem("s_wnat")
        s_row = [sem("s_row0"), sem("s_row1")]
        s_set = sem("s_set")
        s_wT = sem("s_wT"); s_wev = sem("s_wev")
        s_sv = sem("s_sv"); s_sv2 = sem("s_sv2"); s_mid = sem("s_mid")
        s_scl = sem("s_scl"); s_str = sem("s_str"); s_shi = sem("s_shi"); s_slo = sem("s_slo")
        s_mm = sem("s_mm"); s_mmt = sem("s_mmt"); s_mmev = sem("s_mmev"); s_mmst = sem("s_mmst")
        s_dsc = sem("s_dsc"); s_dsl = sem("s_dsl"); s_dtr = sem("s_dtr"); s_dhi = sem("s_dhi"); s_dlo = sem("s_dlo")
        s_xin = sem("s_xin"); s_p1t = sem("s_p1t"); s_xT = sem("s_xT")
        s_p1q = sem("s_p1q"); s_rope = sem("s_rope"); s_pp = sem("s_pp"); s_pp2 = sem("s_pp2"); s_spl2 = sem("s_spl2"); s_qkw = sem("s_qkw")
        s_p1v = sem("s_p1v"); s_vx = sem("s_vx")
        s_stk = [sem("s_stk0"), sem("s_stk1")]
        s_mx = sem("s_mx"); s_red = sem("s_red"); s_spl = sem("s_spl")
        s_mt = sem("s_mt"); s_mr = sem("s_mr")
        s_md = [[sem(f"s_md{p}{r}") for r in range(2)] for p in range(2)]
        s_st = sem("s_st"); s_exp = sem("s_exp"); s_pv = sem("s_pv"); s_yv = sem("s_yv")
        s_yw = [sem("s_yw0"), sem("s_yw1")]; s_yd = sem("s_yd")
        s_xr = sem("s_xr"); s_xb = sem("s_xb"); s_yn = sem("s_yn"); s_yr = sem("s_yr"); s_prj = sem("s_prj")
        s_ln1 = sem("s_ln1"); s_rs1 = sem("s_rs1"); s_x1 = sem("s_x1"); s_x1s = sem("s_x1s")
        s_x1t = sem("s_x1t"); s_x1T = sem("s_x1T"); s_xl = sem("s_xl"); s_gt = sem("s_gt")
        s_rt = sem("s_rt"); s_le = sem("s_le"); s_cb = sem("s_cb"); s_ct = sem("s_ct"); s_cT = sem("s_cT")
        s_cur = sem("s_cur")
        s_g = sem("s_g"); s_u = sem("s_u"); s_bc = sem("s_bc"); s_d = sem("s_d")
        s_si = sem("s_si"); s_t1 = sem("s_t1"); s_t2 = sem("s_t2"); s_hh = sem("s_hh"); s_h = sem("s_h")
        s_ye = sem("s_ye"); s_p5t = sem("s_p5t"); s_xo = sem("s_xo"); s_ln2 = sem("s_ln2")
        s_rs2 = sem("s_rs2"); s_o = sem("s_o"); s_os = sem("s_os")
        s_passed = {nc.vector: sem("s_passed_vector"), nc.gpsimd: sem("s_passed_gpsimd")}

        N_CST = 16 * (3 + 4 * H + 2 + 2)
        N_WNAT = 16 * (4 * H + 3)
        N_SET = 11
        LN = 11
        RT = 11
        CB = 8
        ODD = {"attention": (7, 2), "x": (3, 7), "q": (2, 3), "v": (7, 2), "k": (3, 7), "x1": (2, 3),
               "router": 7, "max": 7, "router weights": 7, "sum": 7}

        def wait(eng, s, per, b, c):
            if isinstance(b, int) and per * b + c <= 0:
                return
            eng.wait_ge(s, b * per + c)

        def wait_apart(eng, s, value):
            if isinstance(value, int):
                if value > 0:
                    eng.wait_ge(s, value)
                return
            eng.wait_ge(s, value)
            eng.sem_inc(s_passed[eng], 1)

        def phases(body):
            body(0)
            body(1)
            with body.engine.Fori(2, NB - 1) as i:
                body(i)
            body(NB - 1)
            body(NB)

        class Iter:
            def __init__(self, engine, phase_a, phase_b):
                self.engine, self.a, self.b = engine, phase_a, phase_b

            def __call__(self, i):
                self.a(i)
                self.b(i)

        def has(i, lo, hi):
            return lo <= i <= hi if isinstance(i, int) else lo <= 2 and hi >= NB - 2

        def dst_v(t):
            return vx[:, t, :, 0:D]

        def su_nat(r):
            return work[:, r * 512:(r + 1) * 512].rearrange("p (m c) -> p m c", m=2)

        def su_scl(r):
            return work[:, 1024 + r * 512:1024 + (r + 1) * 512].rearrange("p (m c) -> p m c", m=2)

        def su_dn(r):
            return work[:, 2048 + r * 256:2048 + (r + 1) * 256].rearrange("p (m f) -> p m f", m=2)

        def su_mm(r):
            return work[:, 2560 + r * 128:2560 + (r + 1) * 128]

        def su_prod(r):
            return su_scl(r)[:, 0, :].rearrange("p (m f) -> p m f", m=2)

        def flat(w, e):
            v = w[:, bass.ds(e, 1)]
            return v.rearrange("p o a b f -> p (o a b f)") if len(w.shape) == 5 else v.rearrange("p o f -> p (o f)")

        def along(v, n):
            return v.rearrange("p (m o) -> p m o", o=1).to_broadcast([P, v.shape[1], n])

        def under(v, m):
            return v.rearrange("p (o n) -> p o n", o=1).to_broadcast([P, m, v.shape[1]])

        def pick1(w, e, *rest):
            if rest:
                return w[:, e, rest[0]:rest[0] + 1] if isinstance(e, int) else \
                    w[:, bass.ds(e, 1), rest[0]:rest[0] + 1].rearrange("p o f -> p (o f)")
            return w[:, e:e + 1] if isinstance(e, int) else w[:, bass.ds(e, 1)]

        block = ctx.enter_context(nc.Block())

        @block.sync
        def _(sp):
            for dst, src in ((ident[:, :], ident_h), (cosT[:, :], cos_t), (sinT[:, :], sin_t)):
                sp.dma_start(dst, src).then_inc(s_cst, 16)
            for dst, src in ((bqc, bq), (bkc, bk)):
                for r in range(2):
                    v = src.rearrange("(h r j) -> h r j", h=H, r=2)[:, r, :].rearrange("h j -> h j")
                    for h in range(H):
                        sp.dma_start(dst[HALF * h:HALF * h + HALF, r:r + 1],
                                     v[h:h + 1, :].rearrange("o j -> j o")).then_inc(s_cst, 16)
            for dst, src in ((bv_b, bv), (bp_b, bp)):
                sp.dma_start(dst[:, :], src.rearrange("(o c) -> o c", o=1).to_broadcast([P, C])).then_inc(s_cst, 16)
            sp.dma_start(x1[:, 0, 0:P], mask_h[0]).then_inc(s_cst, 16)
            sp.dma_start(x1[:, 1, 0:P], mask_h[1]).then_inc(s_cst, 16)
            for n, src in enumerate((wq, wk)):
                for r in range(2):
                    for h in range(H):
                        sp.dma_start(x1Toev[HALF * h:HALF * h + HALF, n, r * C:(r + 1) * C],
                                     src[D * h + HALF * r:D * h + HALF * r + HALF, :]).then_inc(s_wnat, 16)
            sp.dma_start(ono[:, 0:2, :], wv.rearrange("(m p) c -> p m c", p=P)).then_inc(s_wnat, 16)
            sp.dma_start(ono[:, 2:4, :], wp.rearrange("(m p) c -> p m c", p=P)).then_inc(s_wnat, 16)
            sp.dma_start(xin[0:E, 0, :], gate_w).then_inc(s_wnat, 16)

            with sp.Fori(0, E // 2) as n:
                for r in range(2):
                    sp.wait_ge(s_scl, n * 2 + r + 1)
                    sp.dma_start(su_nat(r), gate_up_w[bass.ds(n * 2 + r, 1)].rearrange("o (m p) c -> p (o m) c", p=P)
                                 ).then_inc(s_row[r], 16)
            sp.wait_ge(s_mmev, 1)
            sp.dma_start(mm_dram, xin[0:E, 1, 0:F]).then_inc(s_mmst, 16)
            sp.wait_ge(s_mmst, 16)
            with sp.Fori(0, 2) as rnd:
                with sp.Fori(0, E // 2) as n:
                    for r in range(2):
                        sp.wait_ge(s_dsc, rnd * E + n * 2 + (r + 1))
                        sp.dma_start(su_dn(r), down_w[bass.ds(n * 2 + r, 1)].rearrange("o (m p) f -> p (o m) f", p=P)
                                     ).then_inc(s_row[r], 16)
                        sp.dma_start(su_mm(r), mm_dram[bass.ds(n * 2 + r, 1), :].to_broadcast([P, F])
                                     ).then_inc(s_row[r], 16)

            def stack(b, g, r):
                for n, dst in enumerate((qs, ks)):
                    src = parts_dram[b, n] if isinstance(b, int) else \
                        parts_dram[bass.ds(b, 1), n].rearrange("o r t -> (o r) t")
                    sp.dma_start(dst[0:KS, r, :, :],
                                 src[4 * KS * g:4 * KS * (g + 1), :].rearrange("(h k) t -> k h t", h=4)).then_inc(s_stk[r], 16)

            def max_rows(b, g, p):
                r = g % 2
                wait(sp, s_mr, 8, b, 2 * g + p + 1)
                sp.dma_start(qs[KS:KX, r, 2 * p:2 * p + 2, :], mrow[:, p, :]).then_inc(s_md[p][r], 16)

            def attention_in(b, c):
                if c == 0:
                    wait(sp, s_pp, 2, b, 2)
                    wait(sp, s_prj, 2, b, 0)
                    wait(sp, s_p1v, 2, b, 2)
                    wait(sp, s_p1q, 4, b, 4)
                for r in range(2):
                    wait(sp, s_yw[r], 32, b, 16 * (c + 1))
                for w, dst in ((0, ynum), (1, xTden)):
                    src = att_dram[b, 8 * c:8 * c + 8, w] if isinstance(b, int) else \
                        att_dram[bass.ds(b, 1), 8 * c:8 * c + 8, w].rearrange("o h d t -> (o h) d t")
                    sp.dma_start(dst[:, c, :], src).then_inc(s_yd, 16)

            def phase_a(i):
                if not has(i, 0, NB - 1):
                    return
                wait(sp, s_qkw, 192, i, 192)
                for g in range(2):
                    wait(sp, s_st, 32, i, 8 * (g - 1))
                    stack(i, g, g % 2)
                max_rows(i, 0, 0)
                for g in range(NQ):
                    max_rows(i, g, 1)
                    if g < NQ - 1:
                        max_rows(i, g + 1, 0)
                    if g < NQ - 2:
                        wait(sp, s_st, 32, i, 8 * (g + 1))
                        stack(i, g + 2, g % 2)
                    if g == 2:
                        attention_in(i, 0)
                attention_in(i, 1)

            def phase_b(i):
                if has(i, 0, NB - 2):
                    write_parts(i + 1)

            def write_parts(b):
                for n, runs in enumerate((((0, 3, 0), (3, 2, 0), (5, 1, 0)), ((0, 3, 0), (3, 2, 1), (5, 1, 2)))):
                    wait(sp, s_pp, 2, b, n + 1)
                    dst = parts_dram[b, n] if isinstance(b, int) else \
                        parts_dram[bass.ds(b, 1), n].rearrange("o c t -> (o c) t")
                    dst = dst.rearrange("(p r a) t -> r p a t", r=2, a=6)
                    for half in range(2):
                        for at, count, part in runs:
                            src = pbuf[:, half, part:part + count, :] if n == 0 else \
                                pbuf[:, half, part:part + 1, :].to_broadcast([P, count, T])
                            sp.dma_start(dst[half][:, at:at + count, :], src).then_inc(s_qkw, 16)
            write_parts(0)
            phases(Iter(sp, phase_a, phase_b))


        @block.gpsimd
        def _(pool):
            def load_x(b):
                wait_apart(pool, s_p1t, b * 2 + 0)
                src = x[b] if isinstance(b, int) else x[bass.ds(b, 1)].rearrange("o t c -> (o t) c")
                pool.dma_start(xin[:, :, :], src.rearrange("(n p) c -> p n c", p=P)).then_inc(s_xin, 16)

            def split_parts(b):
                for n in range(2):
                    wait(pool, s_rope, 8, b, 4 * n + 4)
                    nc.gpsimd.tensor_tensor(qf[:, 0, :], qf[:, 0, :], ynum[:, 0, :], ALU.subtract).then_inc(s_pp2, 1)
                    nc.gpsimd.tensor_tensor(qf[:, 1, :], qf[:, 1, :], ynum[:, 1, :], ALU.add).then_inc(s_pp2, 1)
                    wait(pool, s_pp2, 10, b, 5 * n + 2)
                    wait_apart(pool, s_qkw, b * 192 + 96 * n)
                    nc.gpsimd.tensor_scalar(pbuf[:, :, 0, :], qf[:, :, :], 1.0, 0.0, ALU.mult, ALU.add).then_inc(s_pp2, 1)
                    wait(pool, s_pp2, 10, b, 5 * n + 3)
                    nc.gpsimd.tensor_tensor(qf[:, :, :], qf[:, :, :], pbuf[:, :, 0, :], ALU.subtract).then_inc(s_pp2, 1)
                    wait_apart(pool, s_pp2, b * 10 + 5 * n + 4)
                    nc.gpsimd.tensor_scalar(pbuf[:, :, 1, :], qf[:, :, :], 1.0, 0.0, ALU.mult, ALU.add).then_inc(s_pp2, 1)
                    wait(pool, s_pp2, 10, b, 5 * n + 5)
                    nc.gpsimd.tensor_tensor(pbuf[:, :, 2, :], qf[:, :, :], pbuf[:, :, 1, :], ALU.subtract).then_inc(s_pp, 1)

            def rsqrt(which, ln, done, b):
                wait(pool, ln, LN, b, LN)
                nc.gpsimd.tensor_tensor(rs[:, which, :], ve[:, which, :], mhalf[:, :], ALU.pow).then_inc(done, 1)

            pool.wait_ge(s_set, N_SET)
            pool.wait_ge(s_wT, 5)
            pool.wait_ge(s_mmst, 16)
            load_x(0)
            split_parts(0)

            def phase_a(i):
                if has(i, 0, NB - 1):
                    wait(pool, s_x1t, 2, i, 0)
                    wait_apart(pool, s_x1s, i * 16 + 0)
                    src = x[i] if isinstance(i, int) else x[bass.ds(i, 1)].rearrange("o t c -> (o t) c")
                    pool.dma_start(x1[:, :, :], src.rearrange("(n p) c -> p n c", p=P)).then_inc(s_xr, 16)
                if has(i, 0, NB - 2):
                    load_x(i + 1)
                if has(i, 0, NB - 1):
                    wait(pool, s_xr, 16, i, 16)
                    nc.gpsimd.tensor_tensor(x1[:, :, :], x1[:, :, :],
                                            bp_b[:, :].rearrange("p (o c) -> p o c", o=1).to_broadcast([P, NT, C]),
                                            ALU.add).then_inc(s_xb, 1)
                if has(i, 2, NB):
                    reload_x1(i - 2)
                    finish_ln2(i - 2)

            def reload_x1(b):
                wait_apart(pool, s_os, b * 16 + 0)
                src = x1_dram[b] if isinstance(b, int) else x1_dram[bass.ds(b, 1)].rearrange("o t c -> (o t) c")
                pool.dma_start(ono[:, :, :], src.rearrange("(n p) c -> p n c", p=P)).then_inc(s_xo, 16)

            def finish_ln2(b):
                rsqrt(1, s_ln2, s_rs2, b)

            def store(b):
                wait_apart(pool, s_o, b * NT + NT)
                dst = out[b] if isinstance(b, int) else out[bass.ds(b, 1)].rearrange("o t c -> (o t) c")
                pool.dma_start(dst.rearrange("(n p) c -> p n c", p=P), ono[:, :, :]).then_inc(s_os, 16)

            def phase_b(i):
                if has(i, 2, NB):
                    store(i - 2)
                if has(i, 0, NB - 1):
                    rsqrt(0, s_ln1, s_rs1, i)
                    wait_apart(pool, s_x1, i * NT + NT)
                    dst = x1_dram[i] if isinstance(i, int) else x1_dram[bass.ds(i, 1)].rearrange("o t c -> (o t) c")
                    pool.dma_start(dst.rearrange("(n p) c -> p n c", p=P), x1[:, :, :]).then_inc(s_x1s, 16)
                if has(i, 0, NB - 2):
                    split_parts(i + 1)
            phases(Iter(pool, phase_a, phase_b))
            reload_x1(NB - 1)
            finish_ln2(NB - 1)
            store(NB - 1)
            pool.wait_ge(s_os, 16 * NB)
            pool.wait_ge(s_x1s, 16 * NB)
            pool.wait_ge(s_qkw, 192 * NB)

        @block.tensor
        def _(pe):
            mmul = nc.tensor.matmul

            class Odd:
                last = {}

                def take(self, k, i, s, per, off, c):
                    self.free(k, i)
                    self.last[k] = (s, per, off, c)
                    return k

                def free(self, k, i):
                    if k in self.last:
                        s, per, off, c = self.last[k]
                        wait(pe, s, per, i + off, c)

                def next_iteration(self):
                    self.last = {k: (s, per, off - 1, c) for k, (s, per, off, c) in self.last.items()}

            odd = Odd()

            def xpose4(k, src):
                for n in range(4):
                    last = nc.tensor.transpose(ps[:, k, n * P:(n + 1) * P], src(n), ident[:, :])
                return last

            pe.wait_ge(s_cst, N_CST)
            pe.wait_ge(s_wnat, N_WNAT)
            pe.wait_ge(s_set, N_SET)
            for n, m in enumerate((0, 1)):
                xpose4(n, lambda k: x1Toev[:, m, (k % 2) * C + (k // 2) * P:(k % 2) * C + (k // 2) * P + P]).then_inc(s_wT, 1)
            for n in range(2):
                xpose4(2 + n, lambda k: ono[:, 2 * n + k % 2, (k // 2) * P:(k // 2) * P + P]).then_inc(s_wT, 1)
            for n in range(2):
                last = nc.tensor.transpose(ps[:, 4, n * E:(n + 1) * E], xin[0:E, 0, n * P:(n + 1) * P], ident[0:E, 0:E])
            last.then_inc(s_wT, 1)
            with pe.Fori(0, E // 2) as n:
                for r in range(2):
                    pe.wait_ge(s_scl, n * 2 + r + 3)
                    pe.wait_ge(s_slo, n * 2 + r + 1)
                    xpose4(6 + r, lambda k: su_scl(r)[:, k % 2, (k // 2) * P:(k // 2) * P + P]).then_inc(s_str, 1)
            pe.wait_ge(s_mm, 1)
            nc.tensor.transpose(ps[0:E, 5, 0:P], mm[:, :], ident[:, :]).then_inc(s_mmt, 1)
            with pe.Fori(0, E // 2) as n:
                for r in range(2):
                    pe.wait_ge(s_dsl, n * 2 + r + 1)
                    pe.wait_ge(s_slo, n * 2 + (E + r + 1))
                    for k in range(2):
                        last = nc.tensor.transpose(ps[:, 6 + r, k * P:(k + 1) * P], su_scl(r)[:, 0, k * P:(k + 1) * P], ident[:, :])
                    last.then_inc(s_dtr, 1)
            pe.wait_ge(s_slo, 2 * E + 2)
            pe.wait_ge(s_wev, 5)

            def p1_transpose(i, off):
                b = i + off
                wait(pe, s_xin, 16, b, 16)
                for kc in range(NC):
                    k = odd.take(ODD["x"][kc], i, s_xT, 2, off, kc + 1)
                    xpose4(k, lambda n: xin[:, n, kc * P:(kc + 1) * P]).then_inc(s_p1t, 1)

            def p1_qk(i, off, n):
                b = i + off
                wait(pe, s_xT, 2, b, 2)
                w = (wqT, wkT)[n]
                for half in range(2):
                    k = odd.take(ODD["qk"[n]][half], i, s_rope, 8, off, 4 * n + 2 * half + 2)
                    for kc in range(NC):
                        last = mmul(ps[:, k, :], w[:, kc, half * P:(half + 1) * P], xTden[:, kc, :],
                                    start=(kc == 0), stop=(kc == NC - 1))
                    last.then_inc(s_p1q, 1)

            def p1_v(i, off):
                wait(pe, s_xT, 2, i + off, 2)
                for v in range(2):
                    k = odd.take(ODD["v"][v], i, s_vx, 2, off, v + 1)
                    for m in range(2):
                        t = 2 * v + m
                        for kc in range(NC):
                            last = mmul(ps[:, k, m * C:(m + 1) * C], xTden[:, kc, t * P:(t + 1) * P], wvT[:, kc, :],
                                        start=(kc == 0), stop=(kc == NC - 1))
                    last.then_inc(s_p1v, 1)

            def max_unit(i, g, m):
                p, (tt, h0, nh) = m // len(MUNITS), MUNITS[m % len(MUNITS)]
                r, bank, n = g % 2, BANK_S + m % 2, (tt + 1) * P
                if m == 0:
                    wait(pe, s_stk[r], 2 * 32, i, 32 * (g // 2 + 1))
                wait(pe, s_red, NM * NQ, i, NM * g + m - 1)
                for a in range(nh):
                    h = 2 * p + h0 + a
                    mmul(ps[:, bank, a * n:(a + 1) * n], qs[0:KS, r, h, tt * P:(tt + 1) * P], ks[0:KS, r, h, 0:n],
                         start=True, stop=False)
                    last = mmul(ps[:, bank, a * n + tt * P:(a + 1) * n], identb[:, :], maskq[:, :], start=False, stop=True)
                last.then_inc(s_mx, 1)

            def max_transpose(i, g, p):
                wait(pe, s_spl, 8, i, 2 * g + p + 1)
                k = odd.take(ODD["max"], i, s_mr, 8, 0, 2 * g + p + 1)
                o = ps[:, k, :].bitcast(BF16)
                for t in range(NT):
                    last = nc.tensor.transpose(o[0:6, t * P:(t + 1) * P], mp[:, p, t, :, :].rearrange("q a h -> q (a h)"), identb[:, :])
                last.then_inc(s_mt, 1)

            def score_step(i, g, k):
                p, s, r = k // 4, k % 4, g % 2
                if s == 0:
                    wait(pe, s_md[p][r], 32, i, 16 * (g // 2 + 1))
                wait(pe, s_exp, 8 * NQ, i, 8 * g + k - 1)
                n = T - s * P
                for a in range(2):
                    h, bank = 2 * p + a, 2 * (k % 2) + a
                    mmul(ps[:, bank, 0:n], ks[0:KX, r, h, s * P:(s + 1) * P], qs[0:KX, r, h, s * P:T], start=True, stop=False)
                    last = mmul(ps[:, bank, 0:P], identb[:, :], maskk[:, :], start=False, stop=True)
                last.then_inc(s_st, 1)

            def pv(i, g, s):
                wait(pe, s_exp, 8 * NQ, i, 8 * g + 4 + s + 1)
                if g == 0 and s == 0:
                    wait(pe, s_vx, 2, i, 2)
                if s == 0:
                    wait(pe, s_yv, NQ, i, g)
                for j in range(4):
                    last = mmul(ps[32 * j:32 * j + 32, BANK_PV, s * P:T], vx[:, s, 4 * g + j, :],
                                pT[:, j // 2, j % 2, OFF[s]:OFF[s] + T - s * P],
                                start=(s == 0), stop=(s == NT - 1), tile_position=(0, 32 * j))
                last.then_inc(s_pv, 1)

            def phase_a(i):
                if has(i, 2, NB):
                    wait(pe, s_ye, 2, i - 2, 2)
                if has(i, 0, NB - 1):
                    for k in (2, 3):
                        odd.free(k, i)
                    for m in range(NM):
                        max_unit(i, 0, m)
                        if m == NM - 3:
                            max_transpose(i, 0, 0)
                if has(i, 0, NB - 1):
                    for g in range(NQ):
                        nxt = g < NQ - 1
                        units = {0: (0,), 1: (1,), 2: (2, 3), 3: (4, 5), 4: (6,), 5: (7,), 6: (8, 9), 7: (10, 11)}
                        for k in range(8):
                            score_step(i, g, k)
                            if k == 5:
                                pv(i, g, 0)
                            if k == 6:
                                pv(i, g, 1)
                            if nxt:
                                for m in units[k]:
                                    max_unit(i, g + 1, m)
                            if k == 1:
                                max_transpose(i, g, 1)
                            if k == 6 and nxt:
                                max_transpose(i, g + 1, 0)
                        pv(i, g, 2)
                        pv(i, g, 3)
                        if g == 0 and has(i, 1, NB):
                            router_transpose(i, -1)
                        if g in (0, 1) and has(i, 2, NB):
                            sum_transpose(i, -2, g)
                else:
                    router_transpose(i, -1)
                    for v in range(2):
                        sum_transpose(i, -2, v)

            def router_transpose(i, off):
                wait(pe, s_cb, CB, i + off, CB)
                k = odd.take(ODD["router weights"], i, s_cT, 1, off, 1)
                o = ps[:, k, :].bitcast(BF16)
                for t in range(NT):
                    last = nc.tensor.transpose(o[0:3 * E, t * P:(t + 1) * P], cp[:, t, :, :].rearrange("q a e -> q (a e)"), identb[:, :])
                last.then_inc(s_ct, 1)

            def sum_transpose(i, off, v):
                wait(pe, s_ye, 2, i + off, 2)
                k = odd.take(ODD["sum"], i, s_ln2, LN, off, v + 1)
                xpose4(k, lambda n: x1Toev[:, n % 2, (2 * v + n // 2) * P:(2 * v + n // 2 + 1) * P]).then_inc(s_p5t, 1)

            def project(i):
                wait(pe, s_yn, 1, i, 1)
                for v in range(2):
                    k = odd.take(ODD["attention"][v], i, s_ln1, LN, 0, v + 1)
                    for m in range(2):
                        t = 2 * v + m
                        for kc in range(NC):
                            last = mmul(ps[:, k, m * C:(m + 1) * C], ynum[:, kc, t * P:(t + 1) * P], wpT[:, kc, :],
                                        start=(kc == 0), stop=(kc == NC - 1))
                    last.then_inc(s_prj, 1)

            def x1_transpose(i):
                wait(pe, s_x1, NT, i, NT)
                for kc in range(NC):
                    k = odd.take(ODD["x1"][kc], i, s_x1T, 4, 0, 2 * kc + 2)
                    xpose4(k, lambda n: x1[:, n, kc * P:(kc + 1) * P]).then_inc(s_x1t, 1)

            def router(i):
                wait(pe, s_x1T, 4, i, 4)
                k = odd.take(ODD["router"], i, s_rt, RT, 0, 1)
                for t in range(NT):
                    for kc in range(NC):
                        last = mmul(ps[:, k, t * E:(t + 1) * E], x1Toev[:, kc, t * P:(t + 1) * P], gateT[:, kc, :],
                                    start=(kc == 0), stop=(kc == NC - 1))
                last.then_inc(s_gt, 1)

            def hilo(o, w_hi, w_lo, x_hi, x_lo, start, stop):
                n = len(w_hi)
                for k in range(n):
                    mmul(o, w_hi[k], x_hi[k], start=start and k == 0, stop=False)
                    mmul(o, w_lo[k], x_hi[k], start=False, stop=False)
                    last = mmul(o, w_hi[k], x_lo[k], start=False, stop=stop and k == n - 1)
                return last

            def at(w, e, *rest):
                return w[(slice(None), e) + rest] if isinstance(e, int) else \
                    w[(slice(None), bass.ds(e, 1)) + rest].rearrange("p o f -> p (o f)")

            def gate_up(b, e, r):
                for m, (bank, used, done) in enumerate(((BANK_G, s_si, s_g), (BANK_U, s_t1, s_u))):
                    wait(pe, used, E, b, e)
                    hilo(ps[:, bank, :], [at(gu_hi, e, kc, m, slice(None)) for kc in range(NC)],
                         [at(gu_lo, e, kc, m, slice(None)) for kc in range(NC)],
                         [xh[:, kc, :] for kc in range(NC)], [xl[:, kc, :] for kc in range(NC)],
                         True, True).then_inc(done, 1)
                wait(pe, s_t2, E, b, e)
                pick = sel_col(e)
                mmul(ps[:, BANK_BC, :], pick, combT[:, :], start=True, stop=True).then_inc(s_bc, 1)

            def sel_col(e):
                c = selT[:, e:e + 1] if isinstance(e, int) else selT[:, bass.ds(e, 1)]
                return c.to_broadcast([3 * E, P])

            def down(b, e, r, start=False, stop=False):
                wait(pe, s_h, E, b, e + 1)
                for m in range(NC):
                    last = hilo(ps[:, BANK_Y + m, :], [at(dn_hi, e, slice(m * P, (m + 1) * P))],
                                [at(dn_lo, e, slice(m * P, (m + 1) * P))], [hh[:, r, :]], [hl[:, r, :]], start, stop)
                last.then_inc(s_d, 1)

            def pairs(b, lo, hi):
                if hi <= 2:
                    for n in range(lo, hi):
                        for r in range(2):
                            gate_up(b, 2 * n + r, r)
                            if n:
                                down(b, 2 * (n - 1) + r, r, start=(n == 1 and r == 0))
                    return
                with pe.Fori(lo, hi) as n:
                    for r in range(2):
                        gate_up(b, n * 2 + r, r)
                        down(b, n * 2 + (r - 2), r)

            def phase_b(i):
                experts, prj, nxt = has(i, 1, NB), has(i, 0, NB - 1), has(i, 0, NB - 2)
                b = i - 1
                if experts:
                    wait(pe, s_cur, 2, b, 2)
                    wait(pe, s_cT, 1, b, 1)
                    if has(i, 1, NB - 1):
                        wait(pe, s_yv, NQ, i, NQ)
                    pairs(b, 0, 1)
                    pairs(b, 1, 2)
                if prj:
                    project(i)
                if experts:
                    pairs(b, 2, 4)
                if nxt:
                    p1_transpose(i, 1)
                if experts:
                    pairs(b, 4, 6)
                if nxt:
                    p1_qk(i, 1, 0)
                if experts:
                    pairs(b, 6, 8)
                if nxt:
                    p1_v(i, 1)
                if experts:
                    pairs(b, 8, 10)
                if nxt:
                    p1_qk(i, 1, 1)
                if experts:
                    pairs(b, 10, 12)
                if prj:
                    x1_transpose(i)
                if experts:
                    pairs(b, 12, 14)
                if prj:
                    router(i)
                if experts:
                    pairs(b, 14, 16)
                    for r in range(2):
                        down(b, E - 2 + r, r, stop=(r == 1))
                odd.next_iteration()

            p1_transpose(0, 0)
            p1_qk(0, 0, 0)
            p1_v(0, 0)
            p1_qk(0, 0, 1)
            phases(Iter(pe, phase_a, phase_b))
            for v in range(2):
                sum_transpose(NB + 1, -2, v)

        @block.scalar
        def _(act):
            def actv(o, i, f, **k):
                return nc.scalar.activation(o, i, f, **k)

            act.wait_ge(s_set, N_SET)
            for n, dst in enumerate((wqT, wkT, wvT, wpT)):
                act.wait_ge(s_wT, n + 1)
                actv(dst[:, :, :].rearrange("p a b -> p (a b)"), ps[:, n, :], ACT.Copy).then_inc(s_wev, 1)
            act.wait_ge(s_wT, 5)
            actv(gateT[:, :, :].rearrange("p a b -> p (a b)"), ps[:, 4, 0:2 * E], ACT.Copy).then_inc(s_wev, 1)
            with act.Fori(0, E // 2) as n:
                for r in range(2):
                    act.wait_ge(s_str, n * 2 + r + 1)
                    actv(flat(gu_hi, n * 2 + r), ps[:, 6 + r, :], ACT.Copy).then_inc(s_shi, 1)
            act.wait_ge(s_mmt, 1)
            actv(xin[0:E, 1, 0:P], ps[0:E, 5, 0:P], ACT.Copy).then_inc(s_mmev, 1)
            with act.Fori(0, E // 2) as n:
                for r in range(2):
                    act.wait_ge(s_dtr, n * 2 + r + 1)
                    actv(flat(dn_hi, n * 2 + r), ps[:, 6 + r, 0:C], ACT.Copy).then_inc(s_dhi, 1)
            act.wait_ge(s_slo, 2 * E + 2)

            def x_out(b):
                wait(act, s_yn, 1, b, 0)
                wait(act, s_p1v, 2, b, 0)
                wait(act, s_p1q, 4, b, 0)
                for kc in range(NC):
                    wait(act, s_p1t, 2, b, kc + 1)
                    actv(xTden[:, kc, :], ps[:, ODD["x"][kc], :], ACT.Copy).then_inc(s_xT, 1)

            def x1_out(i):
                wait(act, s_cur, 2, i, 0)
                wait(act, s_gt, 1, i, 0)
                wait(act, s_xl, 1, i, 0)
                wait(act, s_p5t, 2, i - 2, 2)
                for kc in range(NC):
                    wait(act, s_x1t, 2, i, kc + 1)
                    actv(x1Toev[:, kc, :], ps[:, ODD["x1"][kc], :], ACT.Copy).then_inc(s_x1T, 1)
                    actv(xh_n[:, kc, :], ps[:, ODD["x1"][kc], :], ACT.Copy).then_inc(s_x1T, 1)

            def sum_out(b):
                wait(act, s_d, E, b, E)
                wait(act, s_p5t, 2, b, 0)
                if not (isinstance(b, int) and b + 1 > NB - 1):
                    wait(act, s_gt, 1, b, 2)
                    wait(act, s_xl, 1, b, 2)
                for m in range(NC):
                    actv(x1Toev[:, m, :], ps[:, BANK_Y + m, :], ACT.Copy, scale=rc[:, m:m + 1]).then_inc(s_ye, 1)

            def router_exp(b):
                wait(act, s_rt, RT, b, RT)
                wait(act, s_cb, CB, b, 0)
                actv(le[:, :, :], lg[:, :, :], ACT.Exp).then_inc(s_le, 1)

            def router_out(b):
                wait(act, s_ct, 1, b, 1)
                wait(act, s_bc, E, b, 0)
                actv(combT[:, :], ps[0:3 * E, ODD["router weights"], :].bitcast(BF16)[:, 0:T], ACT.Copy).then_inc(s_cT, 1)

            def max_out(i, g, p):
                wait(act, s_mt, 8, i, 2 * g + p + 1)
                wait(act, s_md[p][(g + 1) % 2], 32, i, 16 * ((g + 1) // 2))
                actv(mrow[:, p, :], ps[0:6, ODD["max"], :].bitcast(BF16)[:, 0:T], ACT.Copy).then_inc(s_mr, 1)

            def exp_step(i, g, k):
                p, s = k // 4, k % 4
                n = T - s * P
                wait(act, s_st, 8 * NQ, i, 8 * g + k + 1)
                wait(act, s_pv, 4 * NQ, i, 4 * (g - 1) + s + 1)
                actv(pT[:, p, :, OFF[s]:OFF[s] + n], ps[:, 2 * (k % 2):2 * (k % 2) + 2, 0:n], ACT.Exp,
                     scale=float(1.0 / np.sqrt(np.float32(D)))).then_inc(s_exp, 1)

            def attention_out(i, g):
                r = g % 2
                wait(act, s_pv, 4 * NQ, i, 4 * g + 4)
                wait(act, s_yw[r], 32, i, 16 * (g // 2))
                actv(yev[:, r, :], ps[:, BANK_PV, :], ACT.Copy).then_inc(s_yv, 1)
                wait(act, s_yv, NQ, i, g + 1)
                dst = att_dram[i, 4 * g:4 * g + 4] if isinstance(i, int) else \
                    att_dram[bass.ds(i, 1), 4 * g:4 * g + 4].rearrange("o h w d t -> (o h) w d t")
                act.dma_start(dst.rearrange("h w d t -> (h w d) t"), yev[:, r, :]).then_inc(s_yw[r], 16)

            def silu(i, e, r):
                b = i - 1
                wait(act, s_g, E, b, e + 1)
                wait(act, s_t1, E, b, e - 1)
                actv(sg[:, r, :], ps[:, BANK_G, :], ACT.Silu, scale=pick1(mgu, e, 0)).then_inc(s_si, 1)

            def upper(i, e, r):
                b = i - 1
                wait(act, s_t2, E, b, e + 1)
                wait(act, s_d, E, b, e - 1)
                actv(hh[:, r, :], hf[:, r, :], ACT.Copy).then_inc(s_hh, 1)

            def pairs(i, lo, hi):
                def one(n):
                    for r in range(2):
                        silu(i, n * 2 + r, r)
                        if not (isinstance(n, int) and n == 0 and r == 0):
                            upper(i, n * 2 + (r - 1), 1 - r)
                if hi <= 2:
                    one(lo)
                    return
                with act.Fori(lo, hi) as n:
                    one(n)

            def phase_a(i):
                if has(i, 2, NB):
                    sum_out(i - 2)
                if has(i, 1, NB):
                    router_exp(i - 1)
                if not has(i, 0, NB - 1):
                    router_out(i - 1)
                    return
                max_out(i, 0, 0)
                for g in range(NQ):
                    for k in range(8):
                        exp_step(i, g, k)
                        if k == 1:
                            max_out(i, g, 1)
                        if k == 6 and g < NQ - 1:
                            max_out(i, g + 1, 0)
                    attention_out(i, g)
                    if g == 0 and has(i, 1, NB):
                        router_out(i - 1)

            def phase_b(i):
                experts, prj, nxt = has(i, 1, NB), has(i, 0, NB - 1), has(i, 0, NB - 2)
                for lo, hi in ((0, 1), (1, 2), (2, 4), (4, 6), (6, 8), (8, 10), (10, 12), (12, 14), (14, 16)):
                    if experts:
                        pairs(i, lo, hi)
                    if hi == 4 and nxt:
                        x_out(i + 1)
                    if hi == 12 and prj:
                        x1_out(i)
                if experts:
                    upper(i, E - 1, 1)
            x_out(0)
            phases(Iter(act, phase_a, phase_b))
            sum_out(NB - 1)

        @block.vector
        def _(dve):
            V = nc.vector

            dve.wait_ge(s_cst, N_CST)
            V.tensor_copy(identb[:, :], ident[:, :]).then_inc(s_set, 1)
            V.tensor_copy(maskq[:, :], x1[:, 0, 0:P]).then_inc(s_set, 1)
            V.tensor_copy(maskk[:, :], x1[:, 1, 0:P]).then_inc(s_set, 1)
            for n in range(3):
                V.tensor_copy(selT[E * n:E * n + E, :], ident[E * n:E * n + E, E * n:E * n + E]).then_inc(s_set, 1)
            V.memset(ks[KS:KX, :, :, :], 1.0).then_inc(s_set, 1)
            V.memset(vx[:, :, :, D:2 * D], 1.0).then_inc(s_set, 1)
            V.memset(mhalf[:, :], -0.5).then_inc(s_set, 1)
            V.memset(mx2[:, :, :], 0.0).then_inc(s_scl, 2)
            V.memset(rcp[:, :, :], 0.0).then_inc(s_dsc, 2)
            V.memset(gm[:, :, :], 0.0).then_inc(s_slo, 2)
            V.memset(sm[:, :], 0.0).then_inc(s_set, 1)
            V.memset(mm[:, :], 0.0).then_inc(s_set, 1)
            dve.wait_ge(s_set, N_SET)
            dve.wait_ge(s_scl, 2)
            dve.wait_ge(s_dsc, 2)
            dve.wait_ge(s_slo, 2)

            with dve.Fori(0, E // 2) as n:
                for r in range(2):
                    e = n * 2 + r
                    dve.wait_ge(s_row[r], n * 16 + 16)
                    V.tensor_reduce(mx2[:, r, :], su_nat(r), axis=AX.X, op=ALU.max,
                                    apply_absolute_value=True).then_inc(s_sv, 1)
                    dve.wait_ge(s_sv, e * 3 + 1)
                    V.tensor_scalar_max(mgu[:, bass.ds(e, 1), :].rearrange("p o m -> p (o m)"), mx2[:, r, :],
                                        1e-15).then_inc(s_sv, 1)
                    wait_apart(dve, s_sv, e * 3 + 2)
                    V.reciprocal(rcp[:, r, :], mgu[:, bass.ds(e, 1), :].rearrange("p o m -> p (o m)")).then_inc(s_sv, 1)
                    dve.wait_ge(s_sv, e * 3 + 3)
                    V.tensor_tensor(su_scl(r), su_nat(r), along(rcp[:, r, :], C), ALU.mult).then_inc(s_scl, 1)
                for r in range(2):
                    dve.wait_ge(s_shi, n * 2 + r + 1)
                    V.tensor_tensor(flat(gu_lo, n * 2 + r), ps[:, 6 + r, :], flat(gu_hi, n * 2 + r),
                                    ALU.subtract).then_inc(s_slo, 1)
            V.tensor_tensor(mm[:, :], mgu[:, :, 0], mgu[:, :, 1], ALU.mult).then_inc(s_mid, 1)
            V.tensor_scalar(rg4[:, :], mgu[:, :, 0], 4.0, None, ALU.mult).then_inc(s_mid, 1)
            dve.wait_ge(s_mid, 2)
            V.tensor_scalar(mm[:, :], mm[:, :], 4.0, None, ALU.mult).then_inc(s_mm, 1)
            V.reciprocal(rg4[:, :], rg4[:, :]).then_inc(s_mid, 1)
            with dve.Fori(0, E // 2) as n:
                for r in range(2):
                    e = n * 2 + r
                    dve.wait_ge(s_row[r], n * 32 + (16 * (E // 2) + 32))
                    V.tensor_tensor(su_prod(r), su_dn(r), under(su_mm(r), 2), ALU.mult).then_inc(s_dsc, 1)
                    dve.wait_ge(s_dsc, e + 3)
                    V.tensor_reduce(gm[:, :, bass.ds(e, 1)], su_prod(r), axis=AX.X, op=ALU.max,
                                    apply_absolute_value=True).then_inc(s_sv2, 1)
            dve.wait_ge(s_sv2, E)
            V.tensor_reduce(rinv[:, :], gm[:, :, :], axis=AX.X, op=ALU.max).then_inc(s_mid, 1)
            dve.wait_ge(s_mid, 4)
            V.tensor_scalar_max(rc[:, :], rinv[:, :], 1e-30).then_inc(s_mid, 1)
            dve.wait_ge(s_mid, 5)
            V.reciprocal(rinv[:, :], rc[:, :]).then_inc(s_mid, 1)
            dve.wait_ge(s_mid, 6)
            with dve.Fori(0, E // 2) as n:
                for r in range(2):
                    e = n * 2 + r
                    dve.wait_ge(s_row[r], n * 32 + (16 * (E // 2) + 32 * (E // 2) + 32))
                    V.tensor_tensor(su_prod(r), su_dn(r), under(su_mm(r), 2), ALU.mult).then_inc(s_dsc, 1)
                    dve.wait_ge(s_dsc, e + (E + 3))
                    V.tensor_tensor(su_prod(r), su_prod(r), along(rinv[:, :], F), ALU.mult).then_inc(s_dsl, 1)
                for r in range(2):
                    dve.wait_ge(s_dhi, n * 2 + r + 1)
                    V.tensor_tensor(flat(dn_lo, n * 2 + r), ps[:, 6 + r, 0:C], flat(dn_hi, n * 2 + r),
                                    ALU.subtract).then_inc(s_slo, 1)

            def rope(b, n):
                wait(dve, s_pp, 2, b, n)
                if n == 0:
                    wait(dve, s_prj, 2, b, 0)
                bias = (bqc, bkc)[n]
                for half in range(2):
                    k = ODD["qk"[n]][half]
                    wait(dve, s_p1q, 4, b, 2 * n + half + 1)
                    for dst, tab in ((qf[:, half, :], cosT), (ynum[:, 1 - half, :], sinT)):
                        V.scalar_tensor_tensor(out=dst, in0=ps[:, k, :], scalar=bias[:, half:half + 1], in1=tab[:, :],
                                               op0=ALU.add, op1=ALU.mult).then_inc(s_rope, 1)

            def values(b):
                wait(dve, s_pv, 4 * NQ, b, 0)
                for v in range(2):
                    wait(dve, s_p1v, 2, b, v + 1)
                    for m in range(2):
                        ins = V.tensor_tensor(vx[:, 2 * v + m, :, 0:D],
                                              ps[:, ODD["v"][v], m * C:(m + 1) * C].rearrange("p (h d) -> p h d", h=H),
                                              bv_b[:, :].rearrange("p (h d) -> p h d", h=H), ALU.add)
                    ins.then_inc(s_vx, 1)

            def reduce_unit(i, g, m):
                p, (tt, h0, nh) = m // len(MUNITS), MUNITS[m % len(MUNITS)]
                n = (tt + 1) * P
                wait(dve, s_mx, NM * NQ, i, NM * g + m + 1)
                V.tensor_reduce(mn[:, p, tt, h0:h0 + nh],
                                ps[:, BANK_S + m % 2, 0:nh * n].rearrange("p (a n) -> p a n", a=nh),
                                axis=AX.X, op=ALU.max, negate=True).then_inc(s_red, 1)
                if m % len(MUNITS) == len(MUNITS) - 1:
                    split_max(i, g, p)

            def split_max(i, g, p):
                u = 3 * (2 * g + p)
                wait(dve, s_red, NM * NQ, i, NM * g + len(MUNITS) * (p + 1))
                wait(dve, s_mt, 8, i, 2 * (g - 1) + p + 1)
                V.tensor_copy(mp[:, p, :, 0, :], mn[:, p, :, :]).then_inc(s_spl2, 1)
                wait(dve, s_spl2, 24, i, u + 1)
                V.tensor_tensor(mr[:, p, :, :], mn[:, p, :, :], mp[:, p, :, 0, :], ALU.subtract).then_inc(s_spl2, 1)
                wait(dve, s_spl2, 24, i, u + 2)
                V.tensor_copy(mp[:, p, :, 1, :], mr[:, p, :, :]).then_inc(s_spl2, 1)
                wait(dve, s_spl2, 24, i, u + 3)
                V.tensor_tensor(mp[:, p, :, 2, :], mr[:, p, :, :], mp[:, p, :, 1, :], ALU.subtract).then_inc(s_spl, 1)

            def router_weights(b):
                n = [0]

                def step(ins):
                    n[0] += 1
                    ins.then_inc(s_cb, 1)
                    wait(dve, s_cb, CB, b, n[0])
                wait(dve, s_le, 1, b, 1)
                wait(dve, s_ct, 1, b, 0)
                step(V.tensor_tensor(le[:, :, :], le[:, :, :], msk[:, :, :], ALU.mult))
                step(V.tensor_reduce(sm[:, :], le[:, :, :], axis=AX.X, op=ALU.add))
                step(V.reciprocal(sm[:, :], sm[:, :]))
                step(V.tensor_tensor(le[:, :, :], le[:, :, :], along(sm[:, :], E), ALU.mult))
                step(V.tensor_copy(cp[:, :, 0, :], le[:, :, :]))
                step(V.tensor_tensor(le[:, :, :], le[:, :, :], cp[:, :, 0, :], ALU.subtract))
                step(V.tensor_copy(cp[:, :, 1, :], le[:, :, :]))
                step(V.tensor_tensor(cp[:, :, 2, :], le[:, :, :], cp[:, :, 1, :], ALU.subtract))
                assert n[0] == CB

            def router_choice(i):
                wait(dve, s_gt, 1, i, 1)
                V.tensor_copy(lg[:, :, :], ps[:, ODD["router"], 0:NT * E].rearrange("p (t e) -> p t e", t=NT)).then_inc(s_rt, 1)
                wait_apart(dve, s_rt, i * RT + 1)
                for t in range(NT):
                    V.max(v8[:, t, :], lg[:, t, :]).then_inc(s_rt, 1)
                wait_apart(dve, s_rt, i * RT + 1 + NT)
                for t in range(NT):
                    V.match_replace(lg2[:, t, :], v8[:, t, :], lg[:, t, :], -3.0e38).then_inc(s_rt, 1)
                wait(dve, s_rt, RT, i, 1 + 2 * NT)
                V.tensor_tensor(msk[:, :, :], lg2[:, :, :], lg[:, :, :], ALU.not_equal).then_inc(s_rt, 1)
                V.tensor_tensor(lg[:, :, :], lg[:, :, :], along(v8[:, :, 0], E), ALU.subtract).then_inc(s_rt, 1)

            def ln_add(which, b, v):
                s, dst, done, k = ((s_ln1, x1, s_prj, ODD["attention"][v]), (s_ln2, ono, s_p5t, ODD["sum"]))[which]
                wait(dve, done, 2, b, v + 1)
                if v == 0:
                    wait(dve, (s_xb, s_xo)[which], (1, 16)[which], b, (1, 16)[which])
                part = dst[:, 2 * v:2 * v + 2, :].rearrange("p n c -> p (n c)")
                V.tensor_tensor(part, part, ps[:, k, :], ALU.add).then_inc(s, 1)

            def ln_stats(which, b):
                s, dst = ((s_ln1, x1), (s_ln2, ono))[which]
                wait(dve, s, LN, b, 2)
                for t in range(NT):
                    V.bn_stats(st[:, which, t, :], dst[:, t, :]).then_inc(s, 1)
                wait_apart(dve, s, b * LN + 2 + NT)
                for t in range(NT):
                    V.bn_aggr(mv[:, which, t, :], st[:, which, t, :]).then_inc(s, 1)
                wait(dve, s, LN, b, 2 + 2 * NT)
                V.tensor_scalar_add(ve[:, which, :], mv[:, which, :, 1], EPS).then_inc(s, 1)

            def ln_norm(which, b):
                s, dst, rstd = ((s_x1, x1, s_rs1), (s_o, ono, s_rs2))[which]
                wait(dve, rstd, 1, b, 1)
                for t in range(NT):
                    V.tensor_scalar(dst[:, t, :], dst[:, t, :], mv[:, which, t, 0:1], rs[:, which, t:t + 1],
                                    ALU.subtract, ALU.mult).then_inc(s, 1)

            def product(i, e, r):
                b = i - 1
                wait(dve, s_si, E, b, e + 1)
                wait(dve, s_u, E, b, e + 1)
                wait(dve, s_h, E, b, e - 1)
                V.scalar_tensor_tensor(out=hf[:, r, :], in0=sg[:, r, :], scalar=pick1(rg4, e), in1=ps[:, BANK_U, :],
                                       op0=ALU.mult, op1=ALU.mult).then_inc(s_t1, 1)
                wait(dve, s_bc, E, b, e + 1)
                wait(dve, s_t1, E, b, e + 1)
                V.tensor_tensor(hf[:, r, :], hf[:, r, :], ps[:, BANK_BC, :], ALU.mult).then_inc(s_t2, 1)

            def lower(i, e, r):
                b = i - 1
                wait(dve, s_hh, E, b, e + 1)
                wait(dve, s_d, E, b, e - 1)
                V.tensor_tensor(hl[:, r, :], hf[:, r, :], hh[:, r, :], ALU.subtract).then_inc(s_h, 1)

            def pairs(i, lo, hi):
                def one(n):
                    for r in range(2):
                        product(i, n * 2 + r, r)
                        if not (isinstance(n, int) and n == 0 and r == 0):
                            lower(i, n * 2 + (r - 1), 1 - r)
                if hi <= 2:
                    one(lo)
                    return
                with dve.Fori(lo, hi) as n:
                    one(n)

            def phase_a(i):
                if has(i, 1, NB):
                    wait(dve, s_d, E, i - 1, 0)
                    wait(dve, s_x1T, 4, i - 1, 4)
                    wait(dve, s_xl, 1, i - 1, 1)
                    V.tensor_copy(xh[:, :, :], xh_n[:, :, :]).then_inc(s_cur, 1)
                    V.tensor_copy(xl[:, :, :], xl_n[:, :, :]).then_inc(s_cur, 1)
                if not has(i, 0, NB - 1):
                    router_weights(i - 1)
                    for v in range(2):
                        ln_add(1, i - 2, v)
                    ln_stats(1, i - 2)
                    return
                for m in range(NM):
                    reduce_unit(i, 0, m)
                if has(i, 1, NB):
                    router_weights(i - 1)
                for g in range(1, NQ):
                    for m in range(NM):
                        reduce_unit(i, g, m)
                    if has(i, 2, NB) and g < 3:
                        ln_add(1, i - 2, g - 1)
                        if g == 2:
                            ln_stats(1, i - 2)

            def phase_b(i):
                experts, prj, nxt = has(i, 1, NB), has(i, 0, NB - 1), has(i, 0, NB - 2)
                for lo, hi in ((0, 1), (1, 2), (2, 4), (4, 6), (6, 8), (8, 10), (10, 12), (12, 14), (14, 16)):
                    if experts:
                        pairs(i, lo, hi)
                    if hi == 1:
                        if has(i, 2, NB):
                            ln_norm(1, i - 2)
                        if prj:
                            wait(dve, s_yd, 64, i, 64)
                            V.reciprocal(xTden[:, :, :], xTden[:, :, :]).then_inc(s_yr, 1)
                            wait(dve, s_yr, 1, i, 1)
                            V.tensor_tensor(ynum[:, :, :], ynum[:, :, :], xTden[:, :, :], ALU.mult).then_inc(s_yn, 1)
                    if hi == 2 and prj:
                        for v in range(2):
                            ln_add(0, i, v)
                        ln_stats(0, i)
                    if hi == 4 and prj:
                        ln_norm(0, i)
                    if hi == 6 and nxt:
                        rope(i + 1, 0)
                    if hi == 8 and nxt:
                        values(i + 1)
                    if hi == 10 and nxt:
                        rope(i + 1, 1)
                    if hi == 14 and prj:
                        wait(dve, s_x1T, 4, i, 4)
                        V.tensor_tensor(xl_n[:, :, :], x1Toev[:, :, :], xh_n[:, :, :], ALU.subtract).then_inc(s_xl, 1)
                        router_choice(i)
                if experts:
                    lower(i, E - 1, 1)
            rope(0, 0)
            values(0)
            rope(0, 1)
            phases(Iter(dve, phase_a, phase_b))
            for v in range(2):
                ln_add(1, NB - 1, v)
            ln_stats(1, NB - 1)
            ln_norm(1, NB - 1)


def tables():
    i = np.arange(HALF, dtype=np.float32)
    alpha = (np.float32(1.0) / np.power(np.float32(10000.0), np.float32(2.0) * i / np.float32(D))).astype(np.float32)
    ang = np.arange(T, dtype=np.float32)[:, None] * alpha
    rows = np.tile(ang.T, (H, 1))
    cos_t, sin_t = np.cos(rows).astype(np.float32), np.sin(rows).astype(np.float32)
    r = np.arange(P)
    above = np.where(r[None, :] > r[:, None], np.float32(NEG), np.float32(0))
    return {"cos_t": cos_t, "sin_t": sin_t, "ident_h": np.eye(P, dtype=np.float32),
            "mask_h": np.ascontiguousarray(np.stack([above, above.T]))}


_INS = ["L0_attn_x", "L0_attn_wq", "L0_attn_bq", "L0_attn_wk", "L0_attn_bk", "L0_attn_wv", "L0_attn_bv",
        "L0_attn_wp", "L0_attn_bp", "L0_ffn_gate_w", "L0_ffn_gate_up_w", "L0_ffn_down_w"]


def kernel(**inputs):
    import concourse.bacc as _bacc
    from concourse.bass_utils import run_bass_kernel_spmd as _run

    nc = _bacc.Bacc("TRN2", target_bir_lowering=False, num_devices=1)
    arrays = {name: np.ascontiguousarray(inputs[name]) for name in _INS}
    arrays.update(tables())
    args = [nc.dram_tensor(name, a.shape, mybir.dt.from_np(a.dtype), kind="ExternalInput").ap()
            for name, a in arrays.items()]
    out = nc.dram_tensor("out", (B, T, C), F32, kind="ExternalOutput").ap()
    build(nc, *args, out)
    return _run(nc, [arrays], core_ids=[0]).results[0]["out"]
```

```python
from contextlib import ExitStack

import numpy as np

import concourse.bass as bass
import concourse.mybir as mybir

F32 = mybir.dt.float32
BF16 = mybir.dt.bfloat16
F16 = mybir.dt.float16
ALU = mybir.AluOpType
ACT = mybir.ActivationFunctionType
AX = mybir.AxisListType

P = 128
B, T, C = 16, 512, 256
H, D = 16, 16
E, F, TOPK = 32, 128, 8
NT = T // P
NC = C // P
NQ = H // 4
HALF = D // 2
EPS = 1e-5
NEG = -1e30
KS = 6 * D
KX = KS + 3
MUNITS = [(3, h, 1) for h in range(4)] + [(2, h, 1) for h in range(4)] + [(1, 0, 2), (1, 2, 2), (0, 0, 4)]
NM = len(MUNITS)
SLOT_SUM = (1, 2)
SLOT_PROJECT = (5, 6)
SLOT_X = (7, 8)
SLOT_X1 = (12, 13)
SLOT_Q = (9, 10)
SLOT_ROUTER = 14
SLOT_V = (15, 16)
SLOT_K = (17, 18)
SLOT_WEIGHTS = 20
LE = E // NQ
MSLOT = {at: m for m, at in enumerate([(1, 2), (2, 0), (2, 2), (3, 0), (3, 1), (3, 2), (4, 0), (4, 2), (5, 0), (5, 2), (6, 0)])}


def build(nc, x, wq, bq, wk, bk, wv, bv, wp, bp, gate_w, gate_up_w, down_w,
          cos_t, sin_t, ident_h, mask_h, out, NB=B):
    parts_dram = nc.dram_tensor("qk_parts", [B, 2, H * KS, T], BF16, kind="Internal").ap()
    att_dram = nc.dram_tensor("attention", [B, H, 2, D, T], F32, kind="Internal").ap()
    x1_dram = nc.dram_tensor("x1_scratch", [B, T, C], F32, kind="Internal").ap()
    rec_dram = nc.dram_tensor("reciprocals", [B, H, T], F32, kind="Internal").ap()
    mm_dram = nc.dram_tensor("mm_scratch", [E, F], F32, kind="Internal").ap()

    with ExitStack() as ctx:
        def sb(name, shape, dt=F32):
            return ctx.enter_context(nc.sbuf_tensor(name, shape, dt))

        def sem(name):
            return ctx.enter_context(nc.semaphore(name))

        gu_hi = sb("gu_hi", [P, E, NC, 2, F], F16)
        gu_lo = sb("gu_lo", [P, E, NC, 2, F], F16)
        dn_hi = sb("dn_hi", [P, E, C], F16)
        dn_lo = sb("dn_lo", [P, E, C], F16)
        wqT = sb("wqT", [P, NC, C])
        wkT = sb("wkT", [P, NC, C])
        wvT = sb("wvT", [P, NC, C])
        wpT = sb("wpT", [P, NC, C])
        gateT = sb("gateT", [P, NC, E])
        cosT = sb("cosT", [P, T])
        sinT = sb("sinT", [P, T])
        bqc = sb("bqc", [P, 2])
        bkc = sb("bkc", [P, 2])
        bv_b = sb("bv_b", [P, C])
        bp_b = sb("bp_b", [P, C])
        ident = sb("ident", [P, P])
        identb = sb("identb", [P, P], BF16)
        maskq = sb("maskq", [P, P], BF16)
        maskk = sb("maskk", [P, P], BF16)
        mgu = sb("mgu", [P, E, 2])
        mx2 = sb("mx2", [P, 2, 2])
        rcp = sb("rcp", [P, 2, 2])
        rinv = sb("rinv", [P, NC])
        mgh = sb("mgh", [P, E])
        rc = sb("rc", [P, NC])
        mhalf = sb("mhalf", [P, NT])
        qs = sb("qs", [P, 2, 4, T], BF16)
        ks = sb("ks", [P, 2, 4, T], BF16)
        vx = sb("vx", [P, NT, H, 2 * D])
        vn = sb("vn", [P, NT, C])
        work = sb("work", [P, 8 * T])
        pT = work[:, 0:4 * T].rearrange("p (h n) -> p h n", h=4)
        xin = sb("xin", [P, NT, C])
        xTden = sb("xTden", [P, NC, T])
        ynum = sb("ynum", [P, NC, T])
        den = sb("den", [P, H * T // P])
        qf = sb("qf", [P, 2, T])
        pbuf = sb("pbuf", [P, 2, 3, T], BF16)
        yev = sb("yev", [P, 2, T])
        gm = yev[:, 0, 0:NC * E].rearrange("p (m e) -> p m e", m=NC)
        mm = yev[:, 1, 0:E]
        mn = sb("mn", [P, NT, 4])
        mr = sb("mr", [P, NT, 4])
        mp = sb("mp", [P, NT, 3, 4], BF16)
        mrow = sb("mrow", [12, T], BF16)
        x1 = sb("x1", [P, NT, C])
        x1Toev = sb("x1Toev", [P, NC, T])
        xh_n = sb("xh_n", [P, NC, T], F16)
        xl_n = sb("xl_n", [P, NC, T], F16)
        xh = sb("xh", [P, NC, T], F16)
        xl = sb("xl", [P, NC, T], F16)
        combT = sb("combT", [3 * E, T], BF16)
        combT_n = sb("combT_n", [3 * E, T], BF16)
        selT = sb("selT", [3 * E, E], BF16)
        ono = sb("ono", [P, NT, C])
        st = sb("st", [P, 2, NT, 6])
        mv = sb("mv", [P, 2, NT, 2])
        ve = sb("ve", [P, 2, NT])
        rs = sb("rs", [P, 2, NT])
        lg = sb("lg", [P, NT, E])
        lg2 = sb("lg2", [P, NT, E])
        v8 = sb("v8", [P, NT, 8])
        msk, le = lg2, lg
        sm = sb("sm", [P, NT])
        cp = sb("cp", [P, NT, 3, E], BF16)
        hf = work[:, 4 * T:6 * T].rearrange("p (r t) -> p r t", r=2)
        hh = work[:, 6 * T:7 * T].bitcast(F16).rearrange("p (r t) -> p r t", r=2)
        hl = work[:, 7 * T:8 * T].bitcast(F16).rearrange("p (r t) -> p r t", r=2)

        ps = ctx.enter_context(nc.psum_tensor("ps", [P, 8, 512], F32))
        BANK_G, BANK_U, BANK_Y, BANK_ST, BANK_ODD, BANK_PV = 0, 1, 2, 4, 6, 7

        s_cst = sem("s_cst")
        s_wnat = sem("s_wnat")
        s_row = [sem("s_row0"), sem("s_row1")]
        s_set = sem("s_set")
        s_wT = sem("s_wT"); s_wev = sem("s_wev")
        s_sv = sem("s_sv"); s_sv2 = sem("s_sv2"); s_mid = sem("s_mid")
        s_scl = sem("s_scl"); s_str = sem("s_str"); s_shi = sem("s_shi"); s_slo = sem("s_slo")
        s_mm = sem("s_mm"); s_mmt = sem("s_mmt"); s_mmev = sem("s_mmev"); s_mmst = sem("s_mmst")
        s_dsc = sem("s_dsc"); s_dsl = sem("s_dsl"); s_dtr = sem("s_dtr"); s_dhi = sem("s_dhi"); s_dlo = sem("s_dlo")
        s_xin = sem("s_xin"); s_p1t = sem("s_p1t"); s_xT = sem("s_xT")
        s_p1q = sem("s_p1q"); s_rope = sem("s_rope"); s_pp = sem("s_pp"); s_pp2 = sem("s_pp2"); s_spl2 = sem("s_spl2"); s_qkw = sem("s_qkw")
        s_p1v = sem("s_p1v"); s_vx = sem("s_vx"); s_vc = sem("s_vc")
        s_stk = [sem("s_stk0"), sem("s_stk1")]
        s_mx = sem("s_mx"); s_red = sem("s_red"); s_spl = sem("s_spl")
        s_mt = sem("s_mt"); s_mr = sem("s_mr")
        s_md = [sem("s_md0"), sem("s_md1")]
        s_st = sem("s_st"); s_exp = sem("s_exp"); s_pv = sem("s_pv"); s_yv = sem("s_yv")
        s_yw = [sem("s_yw0"), sem("s_yw1")]; s_yd = sem("s_yd"); s_dn = sem("s_dn"); s_rw = sem("s_rw")
        s_xr = sem("s_xr"); s_xb = sem("s_xb"); s_yn = sem("s_yn"); s_yr = sem("s_yr"); s_prj = sem("s_prj")
        s_ln1 = sem("s_ln1"); s_rs1 = sem("s_rs1"); s_x1 = sem("s_x1"); s_x1s = sem("s_x1s")
        s_x1t = sem("s_x1t"); s_x1T = sem("s_x1T"); s_xl = sem("s_xl"); s_gt = sem("s_gt")
        s_rt = sem("s_rt"); s_le = sem("s_le"); s_cb = sem("s_cb"); s_ct = sem("s_ct"); s_cT = sem("s_cT")
        s_cur = sem("s_cur")
        s_g = sem("s_g"); s_u = sem("s_u"); s_bc = sem("s_bc"); s_d = sem("s_d")
        s_th = sem("s_th"); s_t1 = sem("s_t1"); s_t2 = sem("s_t2"); s_t3 = sem("s_t3"); s_hh = sem("s_hh"); s_h = sem("s_h")
        s_ye = sem("s_ye"); s_p5t = sem("s_p5t"); s_xo = sem("s_xo"); s_ln2 = sem("s_ln2")
        s_rs2 = sem("s_rs2"); s_o = sem("s_o"); s_os = sem("s_os")
        s_passed = {nc.vector: sem("s_passed_vector"), nc.gpsimd: sem("s_passed_gpsimd")}

        N_CST = 16 * (3 + 4 * H + 2 + 2)
        N_WNAT = 16 * (4 * H + 3)
        N_SET = 11
        LN = 11
        RT = 11
        CB = 8

        def wait(eng, s, per, b, c):
            if isinstance(b, int) and per * b + c <= 0:
                return
            eng.wait_ge(s, b * per + c)

        def wait_apart(eng, s, value):
            if isinstance(value, int):
                if value > 0:
                    eng.wait_ge(s, value)
                return
            eng.wait_ge(s, value)
            eng.sem_inc(s_passed[eng], 1)

        def iterations(engine, body):
            for i in range(3):
                body(i)
            with engine.Fori(3, NB - 1) as i:
                body(i)
            for i in range(NB - 1, NB + 3):
                body(i)

        def has(i, lo, hi):
            return lo <= i <= hi if isinstance(i, int) else lo <= 3 and hi >= NB - 2

        def su_nat(r):
            return work[:, r * 512:(r + 1) * 512].rearrange("p (m c) -> p m c", m=2)

        def su_scl(r):
            return work[:, 1024 + r * 512:1024 + (r + 1) * 512].rearrange("p (m c) -> p m c", m=2)

        def su_dn(r):
            return work[:, 2048 + r * 256:2048 + (r + 1) * 256].rearrange("p (m f) -> p m f", m=2)

        def su_mm(r):
            return work[:, 2560 + r * 128:2560 + (r + 1) * 128]

        def su_prod(r):
            return su_scl(r)[:, 0, :].rearrange("p (m f) -> p m f", m=2)

        def flat(w, e):
            v = w[:, bass.ds(e, 1)]
            return v.rearrange("p o a b f -> p (o a b f)") if len(w.shape) == 5 else v.rearrange("p o f -> p (o f)")

        def along(v, n):
            return v.rearrange("p (m o) -> p m o", o=1).to_broadcast([P, v.shape[1], n])

        def under(v, m):
            return v.rearrange("p (o n) -> p o n", o=1).to_broadcast([P, m, v.shape[1]])

        def pick1(w, e, *rest):
            if rest:
                return w[:, e, rest[0]:rest[0] + 1] if isinstance(e, int) else \
                    w[:, bass.ds(e, 1), rest[0]:rest[0] + 1].rearrange("p o f -> p (o f)")
            return w[:, e:e + 1] if isinstance(e, int) else w[:, bass.ds(e, 1)]

        block = ctx.enter_context(nc.Block())

        @block.sync
        def _(sp):
            for dst, src in ((ident[:, :], ident_h), (cosT[:, :], cos_t), (sinT[:, :], sin_t)):
                sp.dma_start(dst, src).then_inc(s_cst, 16)
            for dst, src in ((bqc, bq), (bkc, bk)):
                for r in range(2):
                    v = src.rearrange("(h r j) -> h r j", h=H, r=2)[:, r, :].rearrange("h j -> h j")
                    for h in range(H):
                        sp.dma_start(dst[HALF * h:HALF * h + HALF, r:r + 1],
                                     v[h:h + 1, :].rearrange("o j -> j o")).then_inc(s_cst, 16)
            for dst, src in ((bv_b, bv), (bp_b, bp)):
                sp.dma_start(dst[:, :], src.rearrange("(o c) -> o c", o=1).to_broadcast([P, C])).then_inc(s_cst, 16)
            sp.dma_start(x1[:, 0, 0:P], mask_h[0]).then_inc(s_cst, 16)
            sp.dma_start(x1[:, 1, 0:P], mask_h[1]).then_inc(s_cst, 16)
            for n, src in enumerate((wq, wk)):
                for r in range(2):
                    for h in range(H):
                        sp.dma_start(x1Toev[HALF * h:HALF * h + HALF, n, r * C:(r + 1) * C],
                                     src[D * h + HALF * r:D * h + HALF * r + HALF, :]).then_inc(s_wnat, 16)
            sp.dma_start(ono[:, 0:2, :], wv.rearrange("(m p) c -> p m c", p=P)).then_inc(s_wnat, 16)
            sp.dma_start(ono[:, 2:4, :], wp.rearrange("(m p) c -> p m c", p=P)).then_inc(s_wnat, 16)
            sp.dma_start(xin[0:E, 0, :], gate_w).then_inc(s_wnat, 16)

            with sp.Fori(0, E // 2) as n:
                for r in range(2):
                    sp.wait_ge(s_scl, n * 2 + r + 1)
                    sp.dma_start(su_nat(r), gate_up_w[bass.ds(n * 2 + r, 1)].rearrange("o (m p) c -> p (o m) c", p=P)
                                 ).then_inc(s_row[r], 16)
            sp.wait_ge(s_mmev, 1)
            sp.dma_start(mm_dram, xin[0:E, 1, 0:F]).then_inc(s_mmst, 16)
            sp.wait_ge(s_mmst, 16)
            with sp.Fori(0, 2) as rnd:
                with sp.Fori(0, E // 2) as n:
                    for r in range(2):
                        sp.wait_ge(s_dsc, rnd * E + n * 2 + (r + 1))
                        sp.dma_start(su_dn(r), down_w[bass.ds(n * 2 + r, 1)].rearrange("o (m p) f -> p (o m) f", p=P)
                                     ).then_inc(s_row[r], 16)
                        sp.dma_start(su_mm(r), mm_dram[bass.ds(n * 2 + r, 1), :].to_broadcast([P, F])
                                     ).then_inc(s_row[r], 16)

            def stack(b, g, r):
                for n, dst in enumerate((qs, ks)):
                    src = parts_dram[b, n] if isinstance(b, int) else \
                        parts_dram[bass.ds(b, 1), n].rearrange("o r t -> (o r) t")
                    sp.dma_start(dst[0:KS, r, :, :],
                                 src[4 * KS * g:4 * KS * (g + 1), :].rearrange("(h k) t -> k h t", h=4)).then_inc(s_stk[r], 16)

            def max_rows(b, g):
                r = g % 2
                wait(sp, s_mr, 4, b, g + 1)
                sp.dma_start(qs[KS:KX, r, :, :], mrow[:, :]).then_inc(s_md[r], 16)

            def load_stack(b, g):
                if g == 0:
                    wait(sp, s_qkw, 192, b, 192)
                wait(sp, s_st, 32, b, 8 * (g - 1))
                stack(b, g, g % 2)

            def row(w, b):
                return w[b] if isinstance(b, int) else \
                    w[bass.ds(b, 1)].rearrange("o h t -> (o h) t" if len(w.shape) == 3 else "o h w d t -> (o h) w d t")

            def attention_in(b):
                if has(b, 0, NB - 2):
                    wait(sp, s_pp, 2, b + 1, 2)
                wait(sp, s_prj, 2, b, 0)
                wait(sp, s_yw[0], 32, b, 32)
                wait(sp, s_yw[1], 32, b, 32)
                sp.dma_start(den[:, :], row(att_dram, b)[:, 1, 0, :].rearrange("h (c k) -> h c k", c=P // H)).then_inc(s_dn, 16)
                for c in range(NC):
                    sp.dma_start(ynum[:, c, :], row(att_dram, b)[8 * c:8 * c + 8, 0]).then_inc(s_yd, 16)

            def reciprocals_in(b):
                wait(sp, s_yr, 1, b, 1)
                sp.dma_start(row(rec_dram, b), den[:, :]).then_inc(s_rw, 16)
                wait(sp, s_rw, 16, b, 16)
                wait(sp, s_yn, 2, b, 0)
                if has(b, 0, NB - 2):
                    wait(sp, s_p1v, 2, b + 1, 2)
                    wait(sp, s_p1q, 4, b + 1, 4)
                for c in range(NC):
                    src = row(rec_dram, b)[8 * c:8 * c + 8, :].rearrange("h (o t) -> h o t", o=1).to_broadcast([8, D, T])
                    sp.dma_start(xTden[:, c, :], src).then_inc(s_yd, 16)

            def iteration(i):
                attention, nxt = has(i, 0, NB - 1), has(i, 0, NB - 2)
                if attention:
                    load_stack(i, 1)
                if has(i, 1, NB):
                    attention_in(i - 1)
                    reciprocals_in(i - 1)
                for g in range(1, NQ):
                    if attention and g > 1:
                        load_stack(i, g)
                    if g > 1 and nxt:
                        write_parts(i + 1, g - 2)
                    if attention:
                        max_rows(i, g)
                if nxt:
                    load_stack(i + 1, 0)
                if nxt:
                    max_rows(i + 1, 0)

            def write_parts(b, n):
                runs = (((0, 3, 0), (3, 2, 0), (5, 1, 0)), ((0, 3, 0), (3, 2, 1), (5, 1, 2)))[n]
                wait(sp, s_pp, 2, b, n + 1)
                dst = parts_dram[b, n] if isinstance(b, int) else \
                    parts_dram[bass.ds(b, 1), n].rearrange("o c t -> (o c) t")
                dst = dst.rearrange("(p r a) t -> r p a t", r=2, a=6)
                for half in range(2):
                    for at, count, part in runs:
                        src = pbuf[:, half, part:part + count, :] if n == 0 else \
                            pbuf[:, half, part:part + 1, :].to_broadcast([P, count, T])
                        sp.dma_start(dst[half][:, at:at + count, :], src).then_inc(s_qkw, 16)

            write_parts(0, 0)
            write_parts(0, 1)
            load_stack(0, 0)
            max_rows(0, 0)
            iterations(sp, iteration)


        @block.gpsimd
        def _(pool):
            def load_x(b):
                wait_apart(pool, s_p1t, b * 2 + 0)
                src = x[b] if isinstance(b, int) else x[bass.ds(b, 1)].rearrange("o t c -> (o t) c")
                pool.dma_start(xin[:, :, :], src.rearrange("(n p) c -> p n c", p=P)).then_inc(s_xin, 16)

            def split_parts(b):
                for n in range(2):
                    wait(pool, s_rope, 8, b, 4 * n + 4)
                    nc.gpsimd.tensor_tensor(qf[:, 0, :], qf[:, 0, :], ynum[:, 0, :], ALU.subtract).then_inc(s_pp2, 1)
                    nc.gpsimd.tensor_tensor(qf[:, 1, :], qf[:, 1, :], ynum[:, 1, :], ALU.add).then_inc(s_pp2, 1)
                    wait(pool, s_pp2, 10, b, 5 * n + 2)
                    wait_apart(pool, s_qkw, b * 192 + 96 * n)
                    nc.gpsimd.tensor_scalar(pbuf[:, :, 0, :], qf[:, :, :], 1.0, 0.0, ALU.mult, ALU.add).then_inc(s_pp2, 1)
                    wait(pool, s_pp2, 10, b, 5 * n + 3)
                    nc.gpsimd.tensor_tensor(qf[:, :, :], qf[:, :, :], pbuf[:, :, 0, :], ALU.subtract).then_inc(s_pp2, 1)
                    wait_apart(pool, s_pp2, b * 10 + 5 * n + 4)
                    nc.gpsimd.tensor_scalar(pbuf[:, :, 1, :], qf[:, :, :], 1.0, 0.0, ALU.mult, ALU.add).then_inc(s_pp2, 1)
                    wait(pool, s_pp2, 10, b, 5 * n + 5)
                    nc.gpsimd.tensor_tensor(pbuf[:, :, 2, :], qf[:, :, :], pbuf[:, :, 1, :], ALU.subtract).then_inc(s_pp, 1)

            def rsqrt(which, ln, done, b):
                wait(pool, ln, LN, b, LN)
                nc.gpsimd.tensor_tensor(rs[:, which, :], ve[:, which, :], mhalf[:, :], ALU.pow).then_inc(done, 1)

            def ln_norm(which, b):
                s, dst, rstd = ((s_x1, x1, s_rs1), (s_o, ono, s_rs2))[which]
                wait_apart(pool, rstd, b * 1 + 1)
                for t in range(NT):
                    nc.gpsimd.tensor_scalar(dst[:, t, :], dst[:, t, :], mv[:, which, t, 0:1], rs[:, which, t:t + 1],
                                            ALU.subtract, ALU.mult).then_inc(s, 1)

            pool.wait_ge(s_set, N_SET)
            pool.wait_ge(s_wT, 5)
            pool.wait_ge(s_mmst, 16)
            load_x(0)
            split_parts(0)

            def values_in(b):
                wait(pool, s_pv, 4 * NQ, b, 0)
                wait_apart(pool, s_vx, b * 2 + 2)
                nc.gpsimd.tensor_scalar(vx[:, :, :, 0:D].rearrange("p t h d -> p (t h) d"),
                                        vn[:, :, :].rearrange("p t (h d) -> p (t h) d", h=H),
                                        1.0, 0.0, ALU.mult, ALU.add).then_inc(s_vc, 1)

            def residual(b):
                wait(pool, s_x1t, 2, b, 0)
                wait_apart(pool, s_x1s, b * 16 + 0)
                src = x[b] if isinstance(b, int) else x[bass.ds(b, 1)].rearrange("o t c -> (o t) c")
                pool.dma_start(x1[:, :, :], src.rearrange("(n p) c -> p n c", p=P)).then_inc(s_xr, 16)
                wait(pool, s_xr, 16, b, 16)
                nc.gpsimd.tensor_tensor(x1[:, :, :], x1[:, :, :],
                                        bp_b[:, :].rearrange("p (o c) -> p o c", o=1).to_broadcast([P, NT, C]),
                                        ALU.add).then_inc(s_xb, 1)

            def reload_x1(b):
                wait_apart(pool, s_os, b * 16 + 0)
                wait_apart(pool, s_x1s, b * 16 + 16)
                src = x1_dram[b] if isinstance(b, int) else x1_dram[bass.ds(b, 1)].rearrange("o t c -> (o t) c")
                pool.dma_start(ono[:, :, :], src.rearrange("(n p) c -> p n c", p=P)).then_inc(s_xo, 16)

            def store(b):
                wait_apart(pool, s_o, b * NT + NT)
                dst = out[b] if isinstance(b, int) else out[bass.ds(b, 1)].rearrange("o t c -> (o t) c")
                pool.dma_start(dst.rearrange("(n p) c -> p n c", p=P), ono[:, :, :]).then_inc(s_os, 16)

            def store_x1(b):
                wait_apart(pool, s_x1, b * NT + NT)
                dst = x1_dram[b] if isinstance(b, int) else x1_dram[bass.ds(b, 1)].rearrange("o t c -> (o t) c")
                pool.dma_start(dst.rearrange("(n p) c -> p n c", p=P), x1[:, :, :]).then_inc(s_x1s, 16)

            def iteration(i):
                if has(i, 0, NB - 1):
                    values_in(i)
                if has(i, 0, NB - 2):
                    load_x(i + 1)
                if has(i, 3, NB + 2):
                    rsqrt(1, s_ln2, s_rs2, i - 3)
                    ln_norm(1, i - 3)
                    store(i - 3)
                if has(i, 1, NB):
                    rsqrt(0, s_ln1, s_rs1, i - 1)
                    ln_norm(0, i - 1)
                    store_x1(i - 1)
                if has(i, 0, NB - 2):
                    split_parts(i + 1)
                if has(i, 0, NB - 1):
                    residual(i)
                if has(i, 2, NB + 1):
                    reload_x1(i - 2)
            iterations(pool, iteration)
            pool.wait_ge(s_os, 16 * NB)
            pool.wait_ge(s_x1s, 16 * NB)
            pool.wait_ge(s_qkw, 192 * NB)

        @block.tensor
        def _(pe):
            mmul = nc.tensor.matmul

            class Odd:
                last = None

                def take(self, i, s, per, off, c):
                    if self.last:
                        s0, per0, off0, c0 = self.last
                        wait(pe, s0, per0, i + off0, c0)
                    self.last = (s, per, off, c)
                    return BANK_ODD

                def next_iteration(self):
                    s, per, off, c = self.last
                    self.last = (s, per, off - 1, c)

            odd = Odd()

            def xpose4(k, src):
                for n in range(4):
                    last = nc.tensor.transpose(ps[:, k, n * P:(n + 1) * P], src(n), ident[:, :])
                return last

            pe.wait_ge(s_cst, N_CST)
            pe.wait_ge(s_wnat, N_WNAT)
            pe.wait_ge(s_set, N_SET)
            for n, m in enumerate((0, 1)):
                xpose4(n, lambda k: x1Toev[:, m, (k % 2) * C + (k // 2) * P:(k % 2) * C + (k // 2) * P + P]).then_inc(s_wT, 1)
            for n in range(2):
                xpose4(2 + n, lambda k: ono[:, 2 * n + k % 2, (k // 2) * P:(k // 2) * P + P]).then_inc(s_wT, 1)
            for n in range(2):
                last = nc.tensor.transpose(ps[:, 4, n * E:(n + 1) * E], xin[0:E, 0, n * P:(n + 1) * P], ident[0:E, 0:E])
            last.then_inc(s_wT, 1)
            with pe.Fori(0, E // 2) as n:
                for r in range(2):
                    pe.wait_ge(s_scl, n * 2 + r + 3)
                    pe.wait_ge(s_slo, n * 2 + r + 1)
                    xpose4(6 + r, lambda k: su_scl(r)[:, k % 2, (k // 2) * P:(k // 2) * P + P]).then_inc(s_str, 1)
            pe.wait_ge(s_mm, 1)
            nc.tensor.transpose(ps[0:E, 5, 0:P], mm[:, :], ident[:, :]).then_inc(s_mmt, 1)
            with pe.Fori(0, E // 2) as n:
                for r in range(2):
                    pe.wait_ge(s_dsl, n * 2 + r + 1)
                    pe.wait_ge(s_slo, n * 2 + (E + r + 1))
                    for k in range(2):
                        last = nc.tensor.transpose(ps[:, 6 + r, k * P:(k + 1) * P], su_scl(r)[:, 0, k * P:(k + 1) * P], ident[:, :])
                    last.then_inc(s_dtr, 1)
            pe.wait_ge(s_slo, 2 * E + 2)
            pe.wait_ge(s_wev, 5)

            def p1_transpose(i, off, kc):
                wait(pe, s_xin, 16, i + off, 16)
                k = odd.take(i, s_xT, 2, off, kc + 1)
                xpose4(k, lambda n: xin[:, n, kc * P:(kc + 1) * P]).then_inc(s_p1t, 1)

            def p1_qk(i, off, n, half):
                wait(pe, s_xT, 2, i + off, 2)
                w = (wqT, wkT)[n]
                k = odd.take(i, s_rope, 8, off, 4 * n + 2 * half + 2)
                for kc in range(NC):
                    last = mmul(ps[:, k, :], w[:, kc, half * P:(half + 1) * P], xTden[:, kc, :],
                                start=(kc == 0), stop=(kc == NC - 1))
                last.then_inc(s_p1q, 1)

            def p1_v(i, off, v):
                wait(pe, s_xT, 2, i + off, 2)
                k = odd.take(i, s_vx, 2, off, v + 1)
                for m in range(2):
                    t = 2 * v + m
                    for kc in range(NC):
                        last = mmul(ps[:, k, m * C:(m + 1) * C], xTden[:, kc, t * P:(t + 1) * P], wvT[:, kc, :],
                                    start=(kc == 0), stop=(kc == NC - 1))
                last.then_inc(s_p1v, 1)

            def max_unit(i, off, g, m):
                tt, h0, nh = MUNITS[m]
                r, n = g % 2, (tt + 1) * P
                if m == 0:
                    wait(pe, s_stk[r], 2 * 32, i + off, 32 * (g // 2 + 1))
                k = odd.take(i, s_red, NM * NQ, off, NM * g + m + 1)
                for a in range(nh):
                    h = h0 + a
                    mmul(ps[:, k, a * n:(a + 1) * n], qs[0:KS, r, h, tt * P:(tt + 1) * P], ks[0:KS, r, h, 0:n],
                         start=True, stop=False)
                    last = mmul(ps[:, k, a * n + tt * P:(a + 1) * n], identb[:, :], maskq[:, :], start=False, stop=True)
                last.then_inc(s_mx, 1)

            def max_transpose(i, off, g):
                wait(pe, s_spl, 4, i + off, g + 1)
                k = odd.take(i, s_mr, 4, off, g + 1)
                o = ps[:, k, :].bitcast(BF16)
                for t in range(NT):
                    last = nc.tensor.transpose(o[0:12, t * P:(t + 1) * P], mp[:, t, :, :].rearrange("q a h -> q (a h)"), identb[:, :])
                last.then_inc(s_mt, 1)

            def score_step(i, g, k):
                s, p, r = k // 2, k % 2, g % 2
                if k == 0:
                    wait(pe, s_md[r], 32, i, 16 * (g // 2 + 1))
                wait(pe, s_exp, 8 * NQ, i, 8 * g + k)
                n = T - s * P
                for a in range(2):
                    h = 2 * p + a
                    mmul(ps[:, BANK_ST + a, 0:n], ks[0:KX, r, h, s * P:(s + 1) * P], qs[0:KX, r, h, s * P:T],
                         start=True, stop=False)
                    last = mmul(ps[:, BANK_ST + a, 0:P], identb[:, :], maskk[:, :], start=False, stop=True)
                last.then_inc(s_st, 1)

            def pv(i, g, s):
                wait(pe, s_exp, 8 * NQ, i, 8 * g + 2 * s + 2)
                if g == 0 and s == 0:
                    wait(pe, s_vc, 1, i, 1)
                if s == 0:
                    wait(pe, s_yv, NQ, i, g)
                for j in range(4):
                    last = mmul(ps[32 * j:32 * j + 32, BANK_PV, s * P:T], vx[:, s, 4 * g + j, :],
                                pT[:, j, 0:T - s * P],
                                start=(s == 0), stop=(s == NT - 1), tile_position=(0, 32 * j))
                last.then_inc(s_pv, 1)

            def router_transpose(i, off):
                wait(pe, s_cb, CB, i + off, CB)
                k = odd.take(i, s_cT, 1, off, 1)
                o = ps[:, k, :].bitcast(BF16)
                for t in range(NT):
                    last = nc.tensor.transpose(o[0:3 * E, t * P:(t + 1) * P], cp[:, t, :, :].rearrange("q a e -> q (a e)"), identb[:, :])
                last.then_inc(s_ct, 1)

            def sum_transpose(i, off, v):
                wait(pe, s_ye, 2, i + off, 2)
                k = odd.take(i, s_ln2, LN, off, v + 1)
                xpose4(k, lambda n: x1Toev[:, n % 2, (2 * v + n // 2) * P:(2 * v + n // 2 + 1) * P]).then_inc(s_p5t, 1)

            def project(i, off, v):
                wait(pe, s_yn, 2, i + off, 2)
                k = odd.take(i, s_ln1, LN, off, v + 1)
                for m in range(2):
                    t = 2 * v + m
                    for kc in range(NC):
                        last = mmul(ps[:, k, m * C:(m + 1) * C], ynum[:, kc, t * P:(t + 1) * P], wpT[:, kc, :],
                                    start=(kc == 0), stop=(kc == NC - 1))
                last.then_inc(s_prj, 1)

            def x1_transpose(i, off, kc):
                wait(pe, s_x1, NT, i + off, NT)
                k = odd.take(i, s_x1T, 4, off, 2 * kc + 2)
                xpose4(k, lambda n: x1[:, n, kc * P:(kc + 1) * P]).then_inc(s_x1t, 1)

            def router(i, off):
                wait(pe, s_x1T, 4, i + off, 4)
                k = odd.take(i, s_rt, RT, off, 1)
                for t in range(NT):
                    for kc in range(NC):
                        last = mmul(ps[:, k, t * E:(t + 1) * E], x1Toev[:, kc, t * P:(t + 1) * P], gateT[:, kc, :],
                                    start=(kc == 0), stop=(kc == NC - 1))
                last.then_inc(s_gt, 1)

            def hilo(o, w_hi, w_lo, x_hi, x_lo, start, stop):
                n = len(w_hi)
                for k in range(n):
                    mmul(o, w_hi[k], x_hi[k], start=start and k == 0, stop=False)
                    mmul(o, w_lo[k], x_hi[k], start=False, stop=False)
                    last = mmul(o, w_hi[k], x_lo[k], start=False, stop=stop and k == n - 1)
                return last

            def gate_or_up(b, e, m):
                bank, used, done = ((BANK_G, s_t3, s_g), (BANK_U, s_t2, s_u))[m]
                if e == 0 and m == 0:
                    wait(pe, s_cur, 3, b, 3)
                wait(pe, used, E, b, e)
                hilo(ps[:, bank, :], [gu_hi[:, e, kc, m, :] for kc in range(NC)],
                     [gu_lo[:, e, kc, m, :] for kc in range(NC)],
                     [xh[:, kc, :] for kc in range(NC)], [xl[:, kc, :] for kc in range(NC)],
                     True, True).then_inc(done, 1)

            def weights_out(b, e):
                wait(pe, s_t1, E, b, e + 1)
                mmul(ps[:, BANK_G, :], selT[:, e:e + 1].to_broadcast([3 * E, P]), combT[:, :],
                     start=True, stop=True).then_inc(s_bc, 1)

            def down(b, e):
                if e == 0:
                    wait(pe, s_ye, 2, b, 0)
                wait(pe, s_h, E, b, e + 1)
                r = e % 2
                for m in range(NC):
                    last = hilo(ps[:, BANK_Y + m, :], [dn_hi[:, e, m * P:(m + 1) * P]],
                                [dn_lo[:, e, m * P:(m + 1) * P]], [hh[:, r, :]], [hl[:, r, :]], e == 0, e == E - 1)
                last.then_inc(s_d, 1)

            def odd_job(i, e, place):
                last_ln, end, nxt = has(i, 3, NB + 2), has(i, 1, NB), has(i, 0, NB - 2)
                if place == 1:
                    if e in SLOT_SUM and last_ln:
                        sum_transpose(i, -3, SLOT_SUM.index(e))
                    if e in SLOT_PROJECT and end:
                        project(i, -1, SLOT_PROJECT.index(e))
                    if e in SLOT_X and nxt:
                        p1_transpose(i, 1, SLOT_X.index(e))
                    if e in SLOT_X1 and end:
                        x1_transpose(i, -1, SLOT_X1.index(e))
                    if e in SLOT_Q and nxt:
                        p1_qk(i, 1, 0, SLOT_Q.index(e))
                    if e == SLOT_ROUTER and end:
                        router(i, -1)
                    if e in SLOT_V and nxt:
                        p1_v(i, 1, SLOT_V.index(e))
                    if e in SLOT_K and nxt:
                        p1_qk(i, 1, 1, SLOT_K.index(e))
                    if e == SLOT_WEIGHTS and end:
                        router_transpose(i, -1)
                g, le = e // LE, e % LE
                if has(i, 0, NB - 1) if g < NQ - 1 else nxt:
                    off, q = (0, g + 1) if g < NQ - 1 else (1, 0)
                    if (le, place) in MSLOT:
                        max_unit(i, off, q, MSLOT[le, place])
                    if (le, place) == (LE - 1, 0):
                        max_transpose(i, off, q)

            def iteration(i):
                experts, attention, b = has(i, 2, NB + 1), has(i, 0, NB - 1), i - 2
                if has(i, 3, NB + 2):
                    down(b - 1, E - 2)
                if attention:
                    score_step(i, 0, 0)
                for e in range(E):
                    g, le = e // LE, e % LE
                    if experts:
                        gate_or_up(b, e, 0)
                    if attention and e > 0:
                        score_step(i, g, le)
                    odd_job(i, e, 0)
                    if experts:
                        gate_or_up(b, e, 1)
                    odd_job(i, e, 1)
                    if experts:
                        weights_out(b, e)
                    if e == 0 and has(i, 3, NB + 2):
                        down(b - 1, E - 1)
                    if experts and e >= 2:
                        down(b, e - 2)
                    odd_job(i, e, 2)
                    if attention and le % 2:
                        pv(i, g, le // 2)
                odd.next_iteration()

            for kc in range(NC):
                p1_transpose(0, 0, kc)
            for half in range(2):
                p1_qk(0, 0, 0, half)
            for v in range(2):
                p1_v(0, 0, v)
            for half in range(2):
                p1_qk(0, 0, 1, half)
            for m in range(NM):
                max_unit(0, 0, 0, m)
            max_transpose(0, 0, 0)
            iterations(pe, iteration)

        @block.scalar
        def _(act):
            def actv(o, i, f, **k):
                return nc.scalar.activation(o, i, f, **k)

            act.wait_ge(s_set, N_SET)
            for n, dst in enumerate((wqT, wkT, wvT, wpT)):
                act.wait_ge(s_wT, n + 1)
                actv(dst[:, :, :].rearrange("p a b -> p (a b)"), ps[:, n, :], ACT.Copy).then_inc(s_wev, 1)
            act.wait_ge(s_wT, 5)
            actv(gateT[:, :, :].rearrange("p a b -> p (a b)"), ps[:, 4, 0:2 * E], ACT.Copy).then_inc(s_wev, 1)
            with act.Fori(0, E // 2) as n:
                for r in range(2):
                    act.wait_ge(s_str, n * 2 + r + 1)
                    actv(flat(gu_hi, n * 2 + r), ps[:, 6 + r, :], ACT.Copy).then_inc(s_shi, 1)
            act.wait_ge(s_mmt, 1)
            actv(xin[0:E, 1, 0:P], ps[0:E, 5, 0:P], ACT.Copy).then_inc(s_mmev, 1)
            with act.Fori(0, E // 2) as n:
                for r in range(2):
                    act.wait_ge(s_dtr, n * 2 + r + 1)
                    actv(flat(dn_hi, n * 2 + r), ps[:, 6 + r, 0:C], ACT.Copy).then_inc(s_dhi, 1)
            act.wait_ge(s_slo, 2 * E + 2)

            def x_out(b, kc):
                wait(act, s_yn, 2, b, -2)
                wait(act, s_p1v, 2, b, 0)
                wait(act, s_p1q, 4, b, 0)
                wait(act, s_p1t, 2, b, kc + 1)
                actv(xTden[:, kc, :], ps[:, BANK_ODD, :], ACT.Copy).then_inc(s_xT, 1)

            def x1_out(i, kc):
                wait(act, s_cur, 3, i, 0)
                wait(act, s_gt, 1, i, 0)
                wait(act, s_xl, 1, i, 0)
                wait(act, s_p5t, 2, i - 2, 2)
                wait(act, s_x1t, 2, i, kc + 1)
                actv(x1Toev[:, kc, :], ps[:, BANK_ODD, :], ACT.Copy).then_inc(s_x1T, 1)
                actv(xh_n[:, kc, :], ps[:, BANK_ODD, :], ACT.Copy).then_inc(s_x1T, 1)

            def sum_out(b):
                wait(act, s_d, E, b, E)
                if isinstance(b, int):
                    wait(act, s_p5t, 2, b, 0)
                if not (isinstance(b, int) and b + 1 > NB - 1):
                    wait(act, s_gt, 1, b, 2)
                    wait(act, s_xl, 1, b, 2)
                for m in range(NC):
                    actv(x1Toev[:, m, :], ps[:, BANK_Y + m, :], ACT.Copy, scale=rc[:, m:m + 1]).then_inc(s_ye, 1)

            def router_exp(b):
                wait(act, s_rt, RT, b, RT)
                wait(act, s_cb, CB, b, 0)
                actv(le[:, :, :], lg[:, :, :], ACT.Exp).then_inc(s_le, 1)

            def router_out(b):
                wait(act, s_ct, 1, b, 1)
                wait(act, s_cur, 3, b, 0)
                actv(combT_n[:, :], ps[0:3 * E, BANK_ODD, :].bitcast(BF16)[:, 0:T], ACT.Copy).then_inc(s_cT, 1)

            def max_out(b, g):
                wait(act, s_mt, 4, b, g + 1)
                wait(act, s_md[(g + 1) % 2], 32, b, 16 * ((g + 1) // 2))
                actv(mrow[:, :], ps[0:12, BANK_ODD, :].bitcast(BF16)[:, 0:T], ACT.Copy).then_inc(s_mr, 1)

            def exp_step(i, g, k):
                s, p = k // 2, k % 2
                n = T - s * P
                wait(act, s_st, 8 * NQ, i, 8 * g + k + 1)
                wait(act, s_pv, 4 * NQ, i, 4 * g + s)
                actv(pT[:, 2 * p:2 * p + 2, 0:n], ps[:, BANK_ST:BANK_ST + 2, 0:n], ACT.Exp,
                     scale=float(1.0 / np.sqrt(np.float32(D)))).then_inc(s_exp, 1)

            def attention_out(i, g):
                r = g % 2
                wait(act, s_pv, 4 * NQ, i, 4 * g + 4)
                wait(act, s_yw[r], 32, i, 16 * (g // 2))
                actv(yev[:, r, :], ps[:, BANK_PV, :], ACT.Copy).then_inc(s_yv, 1)
                wait(act, s_yv, NQ, i, g + 1)
                dst = att_dram[i, 4 * g:4 * g + 4] if isinstance(i, int) else \
                    att_dram[bass.ds(i, 1), 4 * g:4 * g + 4].rearrange("o h w d t -> (o h) w d t")
                act.dma_start(dst.rearrange("h w d t -> (h w d) t"), yev[:, r, :]).then_inc(s_yw[r], 16)

            def tanh(b, e):
                wait(act, s_g, E, b, e + 1)
                wait(act, s_h, E, b, e - 1)
                actv(hf[:, e % 2, :], ps[:, BANK_G, :], ACT.Tanh, scale=mgh[:, e:e + 1]).then_inc(s_th, 1)

            def upper(b, e):
                wait(act, s_t3, E, b, e + 1)
                wait(act, s_d, E, b, e - 1)
                actv(hh[:, e % 2, :], hf[:, e % 2, :], ACT.Copy).then_inc(s_hh, 1)

            def iteration(i):
                experts, attention, b = has(i, 2, NB + 1), has(i, 0, NB - 1), i - 2
                end, nxt = has(i, 1, NB), has(i, 0, NB - 2)
                for e in range(E):
                    g, le = e // LE, e % LE
                    if experts:
                        tanh(b, e)
                        if e > 0:
                            upper(b, e - 1)
                    if e == 0 and end:
                        attention_out(i - 1, NQ - 1)
                    if attention:
                        if le == 0 and g > 0:
                            attention_out(i, g - 1)
                        exp_step(i, g, le)
                    if e == 0 and has(i, 3, NB + 2):
                        sum_out(i - 3)
                    if le == LE - 1 and (attention if g < NQ - 1 else nxt):
                        if g < NQ - 1:
                            max_out(i, g + 1)
                        else:
                            max_out(i + 1, 0)
                    if e in SLOT_X and nxt:
                        x_out(i + 1, SLOT_X.index(e))
                    if e in SLOT_X1 and end:
                        x1_out(i - 1, SLOT_X1.index(e))
                    if e == SLOT_ROUTER + 2 and end:
                        router_exp(i - 1)
                    if e == SLOT_WEIGHTS and end:
                        router_out(i - 1)
                if experts:
                    upper(b, E - 1)
            for kc in range(NC):
                x_out(0, kc)
            max_out(0, 0)
            iterations(act, iteration)

        @block.vector
        def _(dve):
            V = nc.vector

            dve.wait_ge(s_cst, N_CST)
            V.tensor_copy(identb[:, :], ident[:, :]).then_inc(s_set, 1)
            V.tensor_copy(maskq[:, :], x1[:, 0, 0:P]).then_inc(s_set, 1)
            V.tensor_copy(maskk[:, :], x1[:, 1, 0:P]).then_inc(s_set, 1)
            for n in range(3):
                V.tensor_copy(selT[E * n:E * n + E, :], ident[E * n:E * n + E, E * n:E * n + E]).then_inc(s_set, 1)
            V.memset(ks[KS:KX, :, :, :], 1.0).then_inc(s_set, 1)
            V.memset(vx[:, :, :, D:2 * D], 1.0).then_inc(s_set, 1)
            V.memset(mhalf[:, :], -0.5).then_inc(s_set, 1)
            V.memset(mx2[:, :, :], 0.0).then_inc(s_scl, 2)
            V.memset(rcp[:, :, :], 0.0).then_inc(s_dsc, 2)
            V.memset(gm[:, :, :], 0.0).then_inc(s_slo, 2)
            V.memset(sm[:, :], 0.0).then_inc(s_set, 1)
            V.memset(mm[:, :], 0.0).then_inc(s_set, 1)
            dve.wait_ge(s_set, N_SET)
            dve.wait_ge(s_scl, 2)
            dve.wait_ge(s_dsc, 2)
            dve.wait_ge(s_slo, 2)

            with dve.Fori(0, E // 2) as n:
                for r in range(2):
                    e = n * 2 + r
                    dve.wait_ge(s_row[r], n * 16 + 16)
                    V.tensor_reduce(mx2[:, r, :], su_nat(r), axis=AX.X, op=ALU.max,
                                    apply_absolute_value=True).then_inc(s_sv, 1)
                    dve.wait_ge(s_sv, e * 3 + 1)
                    V.tensor_scalar_max(mgu[:, bass.ds(e, 1), :].rearrange("p o m -> p (o m)"), mx2[:, r, :],
                                        1e-15).then_inc(s_sv, 1)
                    wait_apart(dve, s_sv, e * 3 + 2)
                    V.reciprocal(rcp[:, r, :], mgu[:, bass.ds(e, 1), :].rearrange("p o m -> p (o m)")).then_inc(s_sv, 1)
                    dve.wait_ge(s_sv, e * 3 + 3)
                    V.tensor_tensor(su_scl(r), su_nat(r), along(rcp[:, r, :], C), ALU.mult).then_inc(s_scl, 1)
                for r in range(2):
                    dve.wait_ge(s_shi, n * 2 + r + 1)
                    V.tensor_tensor(flat(gu_lo, n * 2 + r), ps[:, 6 + r, :], flat(gu_hi, n * 2 + r),
                                    ALU.subtract).then_inc(s_slo, 1)
            V.tensor_tensor(mm[:, :], mgu[:, :, 0], mgu[:, :, 1], ALU.mult).then_inc(s_mid, 1)
            V.tensor_scalar(mgh[:, :], mgu[:, :, 0], 0.5, None, ALU.mult).then_inc(s_mid, 1)
            dve.wait_ge(s_mid, 2)
            V.tensor_scalar(mm[:, :], mm[:, :], 4.0, None, ALU.mult).then_inc(s_mm, 1)
            with dve.Fori(0, E // 2) as n:
                for r in range(2):
                    e = n * 2 + r
                    dve.wait_ge(s_row[r], n * 32 + (16 * (E // 2) + 32))
                    V.tensor_tensor(su_prod(r), su_dn(r), under(su_mm(r), 2), ALU.mult).then_inc(s_dsc, 1)
                    dve.wait_ge(s_dsc, e + 3)
                    V.tensor_reduce(gm[:, :, bass.ds(e, 1)], su_prod(r), axis=AX.X, op=ALU.max,
                                    apply_absolute_value=True).then_inc(s_sv2, 1)
            dve.wait_ge(s_sv2, E)
            V.tensor_reduce(rinv[:, :], gm[:, :, :], axis=AX.X, op=ALU.max).then_inc(s_mid, 1)
            dve.wait_ge(s_mid, 3)
            V.tensor_scalar_max(rc[:, :], rinv[:, :], 1e-30).then_inc(s_mid, 1)
            dve.wait_ge(s_mid, 4)
            V.reciprocal(rinv[:, :], rc[:, :]).then_inc(s_mid, 1)
            dve.wait_ge(s_mid, 5)
            with dve.Fori(0, E // 2) as n:
                for r in range(2):
                    e = n * 2 + r
                    dve.wait_ge(s_row[r], n * 32 + (16 * (E // 2) + 32 * (E // 2) + 32))
                    V.tensor_tensor(su_prod(r), su_dn(r), under(su_mm(r), 2), ALU.mult).then_inc(s_dsc, 1)
                    dve.wait_ge(s_dsc, e + (E + 3))
                    V.tensor_tensor(su_prod(r), su_prod(r), along(rinv[:, :], F), ALU.mult).then_inc(s_dsl, 1)
                for r in range(2):
                    dve.wait_ge(s_dhi, n * 2 + r + 1)
                    V.tensor_tensor(flat(dn_lo, n * 2 + r), ps[:, 6 + r, 0:C], flat(dn_hi, n * 2 + r),
                                    ALU.subtract).then_inc(s_slo, 1)

            def rope(b, n, half):
                wait(dve, s_pp, 2, b, n)
                if n == 0:
                    wait(dve, s_prj, 2, b, -2)
                bias = (bqc, bkc)[n]
                wait(dve, s_p1q, 4, b, 2 * n + half + 1)
                for dst, tab in ((qf[:, half, :], cosT), (ynum[:, 1 - half, :], sinT)):
                    V.scalar_tensor_tensor(out=dst, in0=ps[:, BANK_ODD, :], scalar=bias[:, half:half + 1], in1=tab[:, :],
                                           op0=ALU.add, op1=ALU.mult).then_inc(s_rope, 1)

            def values(b, v):
                wait(dve, s_vc, 1, b, 0)
                wait(dve, s_p1v, 2, b, v + 1)
                V.tensor_tensor(vn[:, 2 * v:2 * v + 2, :],
                                ps[:, BANK_ODD, :].rearrange("p (m c) -> p m c", m=2),
                                under(bv_b[:, :], 2), ALU.add).then_inc(s_vx, 1)

            def reduce_unit(b, g, m):
                tt, h0, nh = MUNITS[m]
                n = (tt + 1) * P
                wait(dve, s_mx, NM * NQ, b, NM * g + m + 1)
                V.tensor_reduce(mn[:, tt, h0:h0 + nh],
                                ps[:, BANK_ODD, 0:nh * n].rearrange("p (a n) -> p a n", a=nh),
                                axis=AX.X, op=ALU.max, negate=True).then_inc(s_red, 1)

            def split_max(b, g):
                wait(dve, s_red, NM * NQ, b, NM * g + NM)
                wait(dve, s_mt, 4, b, g)
                V.tensor_copy(mp[:, :, 0, :], mn[:, :, :]).then_inc(s_spl2, 1)
                wait(dve, s_spl2, 12, b, 3 * g + 1)
                V.tensor_tensor(mr[:, :, :], mn[:, :, :], mp[:, :, 0, :], ALU.subtract).then_inc(s_spl2, 1)
                wait(dve, s_spl2, 12, b, 3 * g + 2)
                V.tensor_copy(mp[:, :, 1, :], mr[:, :, :]).then_inc(s_spl2, 1)
                wait(dve, s_spl2, 12, b, 3 * g + 3)
                V.tensor_tensor(mp[:, :, 2, :], mr[:, :, :], mp[:, :, 1, :], ALU.subtract).then_inc(s_spl, 1)

            def router_weights(b):
                n = [0]

                def step(ins):
                    n[0] += 1
                    ins.then_inc(s_cb, 1)
                    wait(dve, s_cb, CB, b, n[0])
                wait(dve, s_le, 1, b, 1)
                wait(dve, s_ct, 1, b, 0)
                step(V.tensor_tensor(le[:, :, :], le[:, :, :], msk[:, :, :], ALU.mult))
                step(V.tensor_reduce(sm[:, :], le[:, :, :], axis=AX.X, op=ALU.add))
                step(V.reciprocal(sm[:, :], sm[:, :]))
                step(V.tensor_tensor(le[:, :, :], le[:, :, :], along(sm[:, :], E), ALU.mult))
                step(V.tensor_copy(cp[:, :, 0, :], le[:, :, :]))
                step(V.tensor_tensor(le[:, :, :], le[:, :, :], cp[:, :, 0, :], ALU.subtract))
                step(V.tensor_copy(cp[:, :, 1, :], le[:, :, :]))
                step(V.tensor_tensor(cp[:, :, 2, :], le[:, :, :], cp[:, :, 1, :], ALU.subtract))
                assert n[0] == CB

            def x1_lower(b):
                wait(dve, s_x1T, 4, b, 4)
                wait(dve, s_cur, 3, b, 0)
                V.tensor_tensor(xl_n[:, :, :], x1Toev[:, :, :], xh_n[:, :, :], ALU.subtract).then_inc(s_xl, 1)

            def router_in(i):
                wait(dve, s_gt, 1, i, 1)
                V.tensor_copy(lg[:, :, :], ps[:, BANK_ODD, 0:NT * E].rearrange("p (t e) -> p t e", t=NT)).then_inc(s_rt, 1)

            def router_choice(i):
                wait_apart(dve, s_rt, i * RT + 1)
                for t in range(NT):
                    V.max(v8[:, t, :], lg[:, t, :]).then_inc(s_rt, 1)
                wait_apart(dve, s_rt, i * RT + 1 + NT)
                for t in range(NT):
                    V.match_replace(lg2[:, t, :], v8[:, t, :], lg[:, t, :], -3.0e38).then_inc(s_rt, 1)
                wait(dve, s_rt, RT, i, 1 + 2 * NT)
                V.tensor_tensor(msk[:, :, :], lg2[:, :, :], lg[:, :, :], ALU.not_equal).then_inc(s_rt, 1)
                V.tensor_tensor(lg[:, :, :], lg[:, :, :], along(v8[:, :, 0], E), ALU.subtract).then_inc(s_rt, 1)

            def ln_add(which, b, v):
                s, dst, done = ((s_ln1, x1, s_prj), (s_ln2, ono, s_p5t))[which]
                wait(dve, done, 2, b, v + 1)
                if v == 0:
                    wait(dve, (s_xb, s_xo)[which], (1, 16)[which], b, (1, 16)[which])
                part = dst[:, 2 * v:2 * v + 2, :].rearrange("p n c -> p (n c)")
                V.tensor_tensor(part, part, ps[:, BANK_ODD, :], ALU.add).then_inc(s, 1)

            def ln_stats(which, b):
                s, dst = ((s_ln1, x1), (s_ln2, ono))[which]
                wait(dve, s, LN, b, 2)
                for t in range(NT):
                    V.bn_stats(st[:, which, t, :], dst[:, t, :]).then_inc(s, 1)
                wait_apart(dve, s, b * LN + 2 + NT)
                for t in range(NT):
                    V.bn_aggr(mv[:, which, t, :], st[:, which, t, :]).then_inc(s, 1)
                wait(dve, s, LN, b, 2 + 2 * NT)
                V.tensor_scalar_add(ve[:, which, :], mv[:, which, :, 1], EPS).then_inc(s, 1)

            def gated(b, e):
                wait(dve, s_th, E, b, e + 1)
                h = hf[:, e % 2, :]
                V.scalar_tensor_tensor(out=h, in0=h, scalar=1.0, in1=ps[:, BANK_G, :],
                                       op0=ALU.add, op1=ALU.mult).then_inc(s_t1, 1)

            def times_up(b, e):
                wait(dve, s_u, E, b, e + 1)
                wait(dve, s_t1, E, b, e + 1)
                h = hf[:, e % 2, :]
                V.scalar_tensor_tensor(out=h, in0=h, scalar=0.125, in1=ps[:, BANK_U, :],
                                       op0=ALU.mult, op1=ALU.mult).then_inc(s_t2, 1)

            def times_weight(b, e):
                wait(dve, s_bc, E, b, e + 1)
                wait(dve, s_t2, E, b, e + 1)
                h = hf[:, e % 2, :]
                V.tensor_tensor(h, h, ps[:, BANK_G, :], ALU.mult).then_inc(s_t3, 1)

            def lower(b, e):
                wait(dve, s_hh, E, b, e + 1)
                wait(dve, s_d, E, b, e - 1)
                V.tensor_tensor(hl[:, e % 2, :], hf[:, e % 2, :], hh[:, e % 2, :], ALU.subtract).then_inc(s_h, 1)

            def reciprocals(b):
                wait(dve, s_dn, 16, b, 16)
                V.reciprocal(den[:, :], den[:, :]).then_inc(s_yr, 1)

            def divide(b, c):
                wait(dve, s_yd, 64, b, 64)
                V.tensor_tensor(ynum[:, c, :], ynum[:, c, :], xTden[:, c, :], ALU.mult).then_inc(s_yn, 1)

            def odd_job(i, e, place):
                last_ln, end, nxt = has(i, 3, NB + 2), has(i, 1, NB), has(i, 0, NB - 2)
                if place == 1:
                    if e in SLOT_SUM and last_ln:
                        ln_add(1, i - 3, SLOT_SUM.index(e))
                    if e in SLOT_PROJECT and end:
                        ln_add(0, i - 1, SLOT_PROJECT.index(e))
                    if e in SLOT_Q and nxt:
                        rope(i + 1, 0, SLOT_Q.index(e))
                    if e == SLOT_ROUTER and end:
                        router_in(i - 1)
                    if e in SLOT_V and nxt:
                        values(i + 1, SLOT_V.index(e))
                    if e in SLOT_K and nxt:
                        rope(i + 1, 1, SLOT_K.index(e))
                g, le = e // LE, e % LE
                if (le, place) in MSLOT:
                    if g < NQ - 1 and has(i, 0, NB - 1):
                        reduce_unit(i, g + 1, MSLOT[le, place])
                    if g == NQ - 1 and nxt:
                        reduce_unit(i + 1, 0, MSLOT[le, place])
                if (le, place) == (LE - 2, 2):
                    if g < NQ - 1 and has(i, 0, NB - 1):
                        split_max(i, g + 1)
                    if g == NQ - 1 and nxt:
                        split_max(i + 1, 0)

            def iteration(i):
                experts, b = has(i, 2, NB + 1), i - 2
                last_ln, end = has(i, 3, NB + 2), has(i, 1, NB)
                if experts:
                    wait(dve, s_u, E, b, 0)
                    wait(dve, s_bc, E, b, 0)
                    wait(dve, s_x1T, 4, b, 4)
                    wait(dve, s_xl, 1, b, 1)
                    wait(dve, s_cT, 1, b, 1)
                    V.tensor_copy(xh[:, :, :], xh_n[:, :, :]).then_inc(s_cur, 1)
                    V.tensor_copy(xl[:, :, :], xl_n[:, :, :]).then_inc(s_cur, 1)
                    V.tensor_copy(combT[:, :], combT_n[:, :]).then_inc(s_cur, 1)
                if last_ln:
                    lower(i - 3, E - 1)
                for e in range(E):
                    odd_job(i, e, 0)
                    if experts:
                        gated(b, e)
                    if experts:
                        times_up(b, e)
                    odd_job(i, e, 1)
                    if experts:
                        times_weight(b, e)
                        if e > 0:
                            lower(b, e - 1)
                    odd_job(i, e, 2)
                    if e == 1 and end:
                        reciprocals(i - 1)
                    if e in (3, 4) and end:
                        divide(i - 1, e - 3)
                    if e == SLOT_SUM[1] and last_ln:
                        ln_stats(1, i - 3)
                    if e == SLOT_PROJECT[1] and end:
                        ln_stats(0, i - 1)
                    if e == SLOT_X1[1] + 1 and end:
                        x1_lower(i - 1)
                    if e == SLOT_ROUTER and end:
                        router_choice(i - 1)
                    if e == SLOT_ROUTER + 3 and end:
                        router_weights(i - 1)

            for half in range(2):
                rope(0, 0, half)
            for v in range(2):
                values(0, v)
            for half in range(2):
                rope(0, 1, half)
            for m in range(NM):
                reduce_unit(0, 0, m)
            split_max(0, 0)
            iterations(dve, iteration)


def tables():
    i = np.arange(HALF, dtype=np.float32)
    alpha = (np.float32(1.0) / np.power(np.float32(10000.0), np.float32(2.0) * i / np.float32(D))).astype(np.float32)
    ang = np.arange(T, dtype=np.float32)[:, None] * alpha
    rows = np.tile(ang.T, (H, 1))
    cos_t, sin_t = np.cos(rows).astype(np.float32), np.sin(rows).astype(np.float32)
    r = np.arange(P)
    above = np.where(r[None, :] > r[:, None], np.float32(NEG), np.float32(0))
    return {"cos_t": cos_t, "sin_t": sin_t, "ident_h": np.eye(P, dtype=np.float32),
            "mask_h": np.ascontiguousarray(np.stack([above, above.T]))}


_INS = ["L0_attn_x", "L0_attn_wq", "L0_attn_bq", "L0_attn_wk", "L0_attn_bk", "L0_attn_wv", "L0_attn_bv",
        "L0_attn_wp", "L0_attn_bp", "L0_ffn_gate_w", "L0_ffn_gate_up_w", "L0_ffn_down_w"]


def kernel(**inputs):
    import concourse.bacc as _bacc
    from concourse.bass_utils import run_bass_kernel_spmd as _run

    nc = _bacc.Bacc("TRN2", target_bir_lowering=False, num_devices=1)
    arrays = {name: np.ascontiguousarray(inputs[name]) for name in _INS}
    arrays.update(tables())
    args = [nc.dram_tensor(name, a.shape, mybir.dt.from_np(a.dtype), kind="ExternalInput").ap()
            for name, a in arrays.items()]
    out = nc.dram_tensor("out", (B, T, C), F32, kind="ExternalOutput").ap()
    build(nc, *args, out)
    return _run(nc, [arrays], core_ids=[0]).results[0]["out"]
```

```python
from contextlib import ExitStack

import numpy as np

import concourse.bass as bass
import concourse.mybir as mybir

F32 = mybir.dt.float32
BF16 = mybir.dt.bfloat16
F16 = mybir.dt.float16
ALU = mybir.AluOpType
ACT = mybir.ActivationFunctionType
AX = mybir.AxisListType

P = 128
B, T, C = 16, 512, 256
H, D = 16, 16
E, F, TOPK = 32, 128, 8
NT = T // P
NC = C // P
NQ = H // 4
HALF = D // 2
EPS = 1e-5
NEG = -1e30
KS = 6 * D
KX = KS + 3
MUNITS = [(3, h, 1) for h in range(4)] + [(2, h, 1) for h in range(4)] + [(1, 0, 2), (1, 2, 2), (0, 0, 4)]
NM = len(MUNITS)
SLOT_SUM = (2, 4)
SLOT_PROJECT = (5, 6)
SLOT_X = (7, 8)
SLOT_X1 = (12, 13)
SLOT_Q = (9, 10)
SLOT_ROUTER = 14
SLOT_V = (17, 18)
SLOT_K = (15, 16)
SLOT_WEIGHTS = 22
SLOT_STATS = ((7, 8), (11, 12))
ODD_SLOTS = SLOT_SUM + SLOT_PROJECT + SLOT_X + SLOT_X1 + SLOT_Q + SLOT_V + SLOT_K + (SLOT_ROUTER, SLOT_WEIGHTS)
LE = E // NQ
PLACES = [(1, 0), (1, 2), (2, 0), (2, 2), (3, 0), (3, 1), (3, 2), (4, 0), (4, 2), (5, 0), (5, 2), (6, 0)]
MSLOT = {at: m for m, at in enumerate(PLACES[1:])}
MSLOT_FIRST = {at: m for m, at in enumerate(PLACES[:-1])}


def build(nc, x, wq, bq, wk, bk, wv, bv, wp, bp, gate_w, gate_up_w, down_w,
          cos_t, sin_t, ident_h, mask_h, out, NB=B):
    parts_dram = nc.dram_tensor("qk_parts", [B, 2, H * KS, T], BF16, kind="Internal").ap()
    att_dram = nc.dram_tensor("attention", [B, H, 2, D, T], F32, kind="Internal").ap()
    x1_dram = nc.dram_tensor("x1_scratch", [B, T, C], F32, kind="Internal").ap()
    rec_dram = nc.dram_tensor("reciprocals", [B, H, T], F32, kind="Internal").ap()

    with ExitStack() as ctx:
        def sb(name, shape, dt=F32):
            return ctx.enter_context(nc.sbuf_tensor(name, shape, dt))

        def sem(name):
            return ctx.enter_context(nc.semaphore(name))

        gu_hi = sb("gu_hi", [P, E, NC, 2, F], F16)
        gu_lo = sb("gu_lo", [P, E, NC, 2, F], F16)
        dn = sb("dn", [P, E, 2, C], F16)
        wqT = sb("wqT", [P, NC, C])
        wkT = sb("wkT", [P, NC, C])
        wvT = sb("wvT", [P, NC, C])
        wpT = sb("wpT", [P, NC, C])
        gateT = sb("gateT", [P, NC, E])
        cosT = sb("cosT", [P, T])
        sinT = sb("sinT", [P, T])
        bqc = sb("bqc", [P, 2])
        bkc = sb("bkc", [P, 2])
        bv_b = sb("bv_b", [P, C])
        bp_b = sb("bp_b", [P, C])
        ident = sb("ident", [P, P])
        identb = sb("identb", [P, P], BF16)
        maskq = sb("maskq", [P, P], BF16)
        maskk = sb("maskk", [P, P], BF16)
        mgu = sb("mgu", [P, E, 2])
        mx2 = sb("mx2", [P, 2, 2])
        rcp = sb("rcp", [P, 2, 2])
        rinv = sb("rinv", [P, NC])
        mgh = sb("mgh", [P, E])
        rc = sb("rc", [P, NC])
        mhalf = sb("mhalf", [P, NT])
        qs = sb("qs", [P, 2, 4, T], BF16)
        ks = sb("ks", [P, 2, 4, T], BF16)
        vx = sb("vx", [P, NT, H, 2 * D])
        vn = sb("vn", [P, NT, C])
        work = sb("work", [P, 8 * T])
        pT = work[:, 0:4 * T].rearrange("p (h n) -> p h n", h=4)
        xin = sb("xin", [P, NT, C])
        xTden = sb("xTden", [P, NC, T])
        ynum = sb("ynum", [P, NC, T])
        den = sb("den", [P, H * T // P])
        qf = sb("qf", [P, 2, T])
        pbuf = sb("pbuf", [P, 2, 3, T], BF16)
        yev = sb("yev", [P, 2, T])
        mn = sb("mn", [P, NT, 4])
        mr = sb("mr", [P, NT, 4])
        mp = sb("mp", [P, NT, 3, 4], BF16)
        mrow = sb("mrow", [12, T], BF16)
        x1 = sb("x1", [P, NT, C])
        x1Toev = sb("x1Toev", [P, NC, T])
        xh_n = sb("xh_n", [P, NC, T], F16)
        xl_n = sb("xl_n", [P, NC, T], F16)
        xh = sb("xh", [P, NC, T], F16)
        xl = sb("xl", [P, NC, T], F16)
        combT = sb("combT", [3 * E, T], BF16)
        combT_n = sb("combT_n", [3 * E, T], BF16)
        selT = sb("selT", [3 * E, E], BF16)
        ono = sb("ono", [P, NT, C])
        mxd = ono[:, 0, :]
        rinvb = ono[:, 1, :]
        mm = ono[:, 2, 0:E]
        rwide = ono[:, 3, :]
        st = sb("st", [P, 2, NT, 6])
        mv = sb("mv", [P, 2, NT, 2])
        ve = sb("ve", [P, 2, NT])
        rs = sb("rs", [P, 2, NT])
        lg = sb("lg", [P, NT, E])
        lg2 = sb("lg2", [P, NT, E])
        v8 = sb("v8", [P, NT, 8])
        msk, le = lg2, lg
        sm = sb("sm", [P, NT])
        cp = sb("cp", [P, NT, 3, E], BF16)
        hf = work[:, 4 * T:6 * T].rearrange("p (r t) -> p r t", r=2)
        hh = work[:, 6 * T:7 * T].bitcast(F16).rearrange("p (r t) -> p r t", r=2)
        hl = work[:, 7 * T:8 * T].bitcast(F16).rearrange("p (r t) -> p r t", r=2)

        ps = ctx.enter_context(nc.psum_tensor("ps", [P, 8, 512], F32))
        BANK_G, BANK_U, BANK_Y, BANK_ST, BANK_ODD, BANK_PV = 0, 1, 2, 4, 6, 7
        BANK_FREE = 3
        FIRST_X, FIRST_QK, FIRST_V = (6, 3), ((6, 3), (0, 1)), (4, 5)

        s_cst = sem("s_cst")
        s_wnat = sem("s_wnat")
        s_row = [sem("s_row0"), sem("s_row1")]
        s_drow = [sem("s_drow0"), sem("s_drow1")]
        s_set = sem("s_set")
        s_wT = sem("s_wT"); s_wev = sem("s_wev")
        s_sv = sem("s_sv"); s_mid = sem("s_mid")
        s_scl = sem("s_scl"); s_str = sem("s_str"); s_shi = sem("s_shi"); s_slo = sem("s_slo")
        s_mm = sem("s_mm"); s_dtr = sem("s_dtr"); s_dev = sem("s_dev"); s_dm = sem("s_dm")
        s_fin = sem("s_fin"); s_rb = sem("s_rb"); s_dsc = sem("s_dsc"); s_dhi = sem("s_dhi"); s_dlo = sem("s_dlo")
        s_xin = sem("s_xin"); s_p1t = sem("s_p1t"); s_xT = sem("s_xT")
        s_p1q = sem("s_p1q"); s_rope = sem("s_rope"); s_pp = sem("s_pp"); s_pp2 = sem("s_pp2"); s_spl2 = sem("s_spl2"); s_qkw = sem("s_qkw")
        s_p1v = sem("s_p1v"); s_vx = sem("s_vx"); s_vc = sem("s_vc")
        s_stk = [sem("s_stk0"), sem("s_stk1")]
        s_mx = sem("s_mx"); s_red = sem("s_red"); s_spl = sem("s_spl")
        s_mt = sem("s_mt"); s_mr = sem("s_mr")
        s_md = [sem("s_md0"), sem("s_md1")]
        s_st = sem("s_st"); s_exp = sem("s_exp"); s_pv = sem("s_pv"); s_yv = sem("s_yv")
        s_yw = [sem("s_yw0"), sem("s_yw1")]; s_yd = sem("s_yd"); s_dn = sem("s_dn"); s_rw = sem("s_rw")
        s_xr = sem("s_xr"); s_xb = sem("s_xb"); s_yn = sem("s_yn"); s_yr = sem("s_yr"); s_prj = sem("s_prj")
        s_ln1 = sem("s_ln1"); s_rs1 = sem("s_rs1"); s_x1 = sem("s_x1"); s_x1s = sem("s_x1s")
        s_x1t = sem("s_x1t"); s_x1T = sem("s_x1T"); s_xl = sem("s_xl"); s_gt = sem("s_gt")
        s_rt = sem("s_rt"); s_le = sem("s_le"); s_cb = sem("s_cb"); s_ct = sem("s_ct"); s_cT = sem("s_cT")
        s_cur = sem("s_cur"); s_ch = sem("s_ch")
        s_g = sem("s_g"); s_u = sem("s_u"); s_bc = sem("s_bc"); s_d = sem("s_d")
        s_th = sem("s_th"); s_t1 = sem("s_t1"); s_t2 = sem("s_t2"); s_t3 = sem("s_t3"); s_hh = sem("s_hh"); s_h = sem("s_h")
        s_ye = sem("s_ye"); s_p5t = sem("s_p5t"); s_xo = sem("s_xo"); s_ln2 = sem("s_ln2")
        s_rs2 = sem("s_rs2"); s_ve = [sem("s_ve1"), sem("s_ve2")]; s_o = sem("s_o"); s_os = sem("s_os")
        s_passed = {nc.vector: sem("s_passed_vector"), nc.gpsimd: sem("s_passed_gpsimd")}

        N_CST = 16 * (3 + 4 + 2 + 2)
        N_WNAT = 16 * (4 + 3)
        N_SET = 9
        LN = 10
        RT = 11
        CB = 8

        def wait(eng, s, per, b, c):
            if isinstance(b, int) and per * b + c <= 0:
                return
            eng.wait_ge(s, b * per + c)

        def wait_apart(eng, s, value):
            if isinstance(value, int):
                if value > 0:
                    eng.wait_ge(s, value)
                return
            eng.wait_ge(s, value)
            eng.sem_inc(s_passed[eng], 1)

        def iterations(engine, body):
            for i in range(3):
                body(i)
            with engine.Fori(3, NB - 1) as i:
                body(i)
            for i in range(NB - 1, NB + 3):
                body(i)

        def has(i, lo, hi):
            return lo <= i <= hi if isinstance(i, int) else lo <= 3 and hi >= NB - 2

        def rows_gu(r):
            return work[:, 4 * T + r * 512:4 * T + (r + 1) * 512].rearrange("p (m c) -> p m c", m=2)

        def rows_dn(r):
            return work[:, 6 * T + r * 256:6 * T + (r + 1) * 256].rearrange("p (m f) -> p m f", m=2)

        def sizes(r):
            return (rinvb, rwide)[r]

        def scaled(r):
            return work[:, 4 * T + r * 512:4 * T + (r + 1) * 512].rearrange("p (e c) -> p e c", e=2)

        def products(e, n):
            return dn[:, e:e + n, :, :].rearrange("p e a c -> p e (a c)").bitcast(F32)

        def load_rows(eng, e):
            eng.dma_start(rows_gu(e % 2), gate_up_w[e].rearrange("(m p) c -> p m c", p=P)).then_inc(s_row[e % 2], 16)
            eng.dma_start(rows_dn(e % 2), down_w[e].rearrange("(m p) f -> p m f", p=P)).then_inc(s_drow[e % 2], 16)

        def max_slots(i):
            if isinstance(i, int) and i < 2:
                return MSLOT_FIRST, (LE - 3, 2), (LE - 2, 2)
            return MSLOT, (LE - 2, 2), (LE - 1, 0)

        def max_bank(i, place):
            if isinstance(i, int) and i < 2 and place == 0:
                return BANK_FREE
            return BANK_Y if isinstance(i, int) and i == 1 and place == 2 else BANK_ODD

        def along(v, n):
            return v.rearrange("p (m o) -> p m o", o=1).to_broadcast([P, v.shape[1], n])

        def under(v, m):
            return v.rearrange("p (o n) -> p o n", o=1).to_broadcast([P, m, v.shape[1]])

        block = ctx.enter_context(nc.Block())

        @block.sync
        def _(sp):
            for dst, src in ((ident[:, :], ident_h), (cosT[:, :], cos_t), (sinT[:, :], sin_t)):
                sp.dma_start(dst, src).then_inc(s_cst, 16)
            for dst, src in ((bqc, bq), (bkc, bk)):
                for r in range(2):
                    sp.dma_start(dst[:, r:r + 1], src.rearrange("(h r j o) -> r h j o", h=H, r=2, o=1)[r]).then_inc(s_cst, 16)
            for dst, src in ((bv_b, bv), (bp_b, bp)):
                sp.dma_start(dst[:, :], src.rearrange("(o c) -> o c", o=1).to_broadcast([P, C])).then_inc(s_cst, 16)
            sp.dma_start(x1[:, 0, 0:P], mask_h[0]).then_inc(s_cst, 16)
            sp.dma_start(x1[:, 1, 0:P], mask_h[1]).then_inc(s_cst, 16)
            for n, src in enumerate((wq, wk)):
                for r in range(2):
                    sp.dma_start(x1Toev[:, n, r * C:(r + 1) * C],
                                 src.rearrange("(h r j) c -> r h j c", h=H, r=2)[r]).then_inc(s_wnat, 16)
            sp.dma_start(ono[:, 0:2, :], wv.rearrange("(m p) c -> p m c", p=P)).then_inc(s_wnat, 16)
            sp.dma_start(ono[:, 2:4, :], wp.rearrange("(m p) c -> p m c", p=P)).then_inc(s_wnat, 16)
            sp.dma_start(vn[0:E, 0, :], gate_w).then_inc(s_wnat, 16)
            for e in range(2):
                load_rows(sp, e)

            def stack(b, g, r):
                for n, dst in enumerate((qs, ks)):
                    src = parts_dram[b, n] if isinstance(b, int) else \
                        parts_dram[bass.ds(b, 1), n].rearrange("o r t -> (o r) t")
                    sp.dma_start(dst[0:KS, r, :, :],
                                 src[4 * KS * g:4 * KS * (g + 1), :].rearrange("(h k) t -> k h t", h=4)).then_inc(s_stk[r], 16)

            def max_rows(b, g):
                r = g % 2
                wait(sp, s_mr, 4, b, g + 1)
                sp.dma_start(qs[KS:KX, r, :, :], mrow[:, :]).then_inc(s_md[r], 16)

            def load_stack(b, g):
                if g == 0:
                    wait(sp, s_qkw, 192, b, 192)
                wait(sp, s_st, 32, b, 8 * (g - 1))
                stack(b, g, g % 2)

            def row(w, b):
                return w[b] if isinstance(b, int) else \
                    w[bass.ds(b, 1)].rearrange("o h t -> (o h) t" if len(w.shape) == 3 else "o h w d t -> (o h) w d t")

            def attention_in(b):
                if has(b, 0, NB - 2):
                    wait(sp, s_pp, 2, b + 1, 2)
                wait(sp, s_prj, 2, b, 0)
                wait(sp, s_yw[0], 32, b, 32)
                wait(sp, s_yw[1], 32, b, 32)
                sp.dma_start(den[:, :], row(att_dram, b)[:, 1, 0, :].rearrange("h (c k) -> h c k", c=P // H)).then_inc(s_dn, 16)
                for c in range(NC):
                    sp.dma_start(ynum[:, c, :], row(att_dram, b)[8 * c:8 * c + 8, 0]).then_inc(s_yd, 16)

            def reciprocals_in(b):
                wait(sp, s_yr, 1, b, 1)
                sp.dma_start(row(rec_dram, b), den[:, :]).then_inc(s_rw, 16)
                wait(sp, s_rw, 16, b, 16)
                wait(sp, s_yn, 2, b, 0)
                if has(b, 0, NB - 2):
                    wait(sp, s_p1v, 2, b + 1, 2)
                    wait(sp, s_p1q, 4, b + 1, 4)
                for c in range(NC):
                    src = row(rec_dram, b)[8 * c:8 * c + 8, :].rearrange("h (o t) -> h o t", o=1).to_broadcast([8, D, T])
                    sp.dma_start(xTden[:, c, :], src).then_inc(s_yd, 16)

            def iteration(i):
                attention, nxt = has(i, 0, NB - 1), has(i, 0, NB - 2)
                if attention:
                    load_stack(i, 1)
                if has(i, 1, NB):
                    attention_in(i - 1)
                    reciprocals_in(i - 1)
                for g in range(1, NQ):
                    if attention and g > 1:
                        load_stack(i, g)
                    if g > 1 and nxt:
                        write_parts(i + 1, g - 2)
                    if attention:
                        max_rows(i, g)
                if nxt:
                    load_stack(i + 1, 0)
                if nxt:
                    max_rows(i + 1, 0)

            def write_parts(b, n):
                runs = (((0, 3, 0), (3, 2, 0), (5, 1, 0)), ((0, 3, 0), (3, 2, 1), (5, 1, 2)))[n]
                wait(sp, s_pp, 2, b, n + 1)
                dst = parts_dram[b, n] if isinstance(b, int) else \
                    parts_dram[bass.ds(b, 1), n].rearrange("o c t -> (o c) t")
                dst = dst.rearrange("(p r a) t -> r p a t", r=2, a=6)
                for half in range(2):
                    for at, count, part in runs:
                        src = pbuf[:, half, part:part + count, :] if n == 0 else \
                            pbuf[:, half, part:part + 1, :].to_broadcast([P, count, T])
                        sp.dma_start(dst[half][:, at:at + count, :], src).then_inc(s_qkw, 16)

            write_parts(0, 0)
            write_parts(0, 1)
            load_stack(0, 0)
            max_rows(0, 0)
            iterations(sp, iteration)


        @block.gpsimd
        def _(pool):
            def load_x(b):
                wait_apart(pool, s_p1t, b * 2 + 0)
                src = x[b] if isinstance(b, int) else x[bass.ds(b, 1)].rearrange("o t c -> (o t) c")
                pool.dma_start(xin[:, :, :], src.rearrange("(n p) c -> p n c", p=P)).then_inc(s_xin, 16)

            def x1_lower(b):
                wait(pool, s_x1T, 4, b, 4)
                wait(pool, s_cur, 2, b, 0)
                nc.gpsimd.tensor_tensor(xl_n[:, :, :], x1Toev[:, :, :], xh_n[:, :, :], ALU.subtract).then_inc(s_xl, 1)

            def split_parts(b, n):
                wait(pool, s_rope, 8, b, 4 * n + 4)
                nc.gpsimd.tensor_tensor(qf[:, 0, :], qf[:, 0, :], ynum[:, 0, :], ALU.subtract).then_inc(s_pp2, 1)
                nc.gpsimd.tensor_tensor(qf[:, 1, :], qf[:, 1, :], ynum[:, 1, :], ALU.add).then_inc(s_pp2, 1)
                wait(pool, s_pp2, 10, b, 5 * n + 2)
                wait_apart(pool, s_qkw, b * 192 + 96 * n)
                nc.gpsimd.tensor_scalar(pbuf[:, :, 0, :], qf[:, :, :], 1.0, 0.0, ALU.mult, ALU.add).then_inc(s_pp2, 1)
                wait(pool, s_pp2, 10, b, 5 * n + 3)
                nc.gpsimd.tensor_tensor(qf[:, :, :], qf[:, :, :], pbuf[:, :, 0, :], ALU.subtract).then_inc(s_pp2, 1)
                wait_apart(pool, s_pp2, b * 10 + 5 * n + 4)
                nc.gpsimd.tensor_scalar(pbuf[:, :, 1, :], qf[:, :, :], 1.0, 0.0, ALU.mult, ALU.add).then_inc(s_pp2, 1)
                wait(pool, s_pp2, 10, b, 5 * n + 5)
                nc.gpsimd.tensor_tensor(pbuf[:, :, 2, :], qf[:, :, :], pbuf[:, :, 1, :], ALU.subtract).then_inc(s_pp, 1)

            def rsqrt(which, ln, done, b):
                wait_apart(pool, ln, b * LN + LN)
                nc.gpsimd.tensor_scalar(ve[:, which, :], mv[:, which, :, 1], 1.0, EPS, ALU.mult, ALU.add).then_inc(s_ve[which], 1)
                wait(pool, s_ve[which], 1, b, 1)
                nc.gpsimd.tensor_tensor(rs[:, which, :], ve[:, which, :], mhalf[:, :], ALU.pow).then_inc(done, 1)

            def ln_norm(which, b):
                s, dst, rstd = ((s_x1, x1, s_rs1), (s_o, ono, s_rs2))[which]
                wait_apart(pool, rstd, b * 1 + 1)
                for t in range(NT):
                    nc.gpsimd.tensor_scalar(dst[:, t, :], dst[:, t, :], mv[:, which, t, 0:1], rs[:, which, t:t + 1],
                                            ALU.subtract, ALU.mult).then_inc(s, 1)

            load_x(0)
            pool.wait_ge(s_set, N_SET)

            def values_in(b):
                wait(pool, s_pv, 4 * NQ, b, 0)
                wait_apart(pool, s_vx, b * 2 + 2)
                nc.gpsimd.tensor_scalar(vx[:, :, :, 0:D].rearrange("p t h d -> p (t h) d"),
                                        vn[:, :, :].rearrange("p t (h d) -> p (t h) d", h=H),
                                        1.0, 0.0, ALU.mult, ALU.add).then_inc(s_vc, 1)

            def residual(b):
                wait(pool, s_x1t, 2, b, 0)
                wait_apart(pool, s_x1s, b * 16 + 0)
                src = x[b] if isinstance(b, int) else x[bass.ds(b, 1)].rearrange("o t c -> (o t) c")
                pool.dma_start(x1[:, :, :], src.rearrange("(n p) c -> p n c", p=P)).then_inc(s_xr, 16)
                wait(pool, s_xr, 16, b, 16)
                nc.gpsimd.tensor_tensor(x1[:, :, :], x1[:, :, :],
                                        bp_b[:, :].rearrange("p (o c) -> p o c", o=1).to_broadcast([P, NT, C]),
                                        ALU.add).then_inc(s_xb, 1)

            def reload_x1(b):
                wait_apart(pool, s_os, b * 16 + 0)
                wait_apart(pool, s_x1s, b * 16 + 16)
                src = x1_dram[b] if isinstance(b, int) else x1_dram[bass.ds(b, 1)].rearrange("o t c -> (o t) c")
                pool.dma_start(ono[:, :, :], src.rearrange("(n p) c -> p n c", p=P)).then_inc(s_xo, 16)

            def store(b):
                wait_apart(pool, s_o, b * NT + NT)
                dst = out[b] if isinstance(b, int) else out[bass.ds(b, 1)].rearrange("o t c -> (o t) c")
                pool.dma_start(dst.rearrange("(n p) c -> p n c", p=P), ono[:, :, :]).then_inc(s_os, 16)

            def store_x1(b):
                wait_apart(pool, s_x1, b * NT + NT)
                dst = x1_dram[b] if isinstance(b, int) else x1_dram[bass.ds(b, 1)].rearrange("o t c -> (o t) c")
                pool.dma_start(dst.rearrange("(n p) c -> p n c", p=P), x1[:, :, :]).then_inc(s_x1s, 16)

            def iteration(i):
                if has(i, 0, NB - 1):
                    values_in(i)
                if has(i, 0, NB - 2):
                    load_x(i + 1)
                if has(i, 1, NB):
                    rsqrt(0, s_ln1, s_rs1, i - 1)
                    ln_norm(0, i - 1)
                    store_x1(i - 1)
                if has(i, 0, NB - 2):
                    split_parts(i + 1, 0)
                if has(i, 1, NB):
                    x1_lower(i - 1)
                if has(i, 3, NB + 2):
                    rsqrt(1, s_ln2, s_rs2, i - 3)
                    if not (isinstance(i, int) and i == NB + 2):
                        ln_norm(1, i - 3)
                    store(i - 3)
                if has(i, 0, NB - 2):
                    split_parts(i + 1, 1)
                if has(i, 0, NB - 1):
                    residual(i)
                if isinstance(i, int) and i == 2:
                    pool.wait_ge(s_dlo, E // 2)
                if has(i, 2, NB + 1):
                    reload_x1(i - 2)
            iterations(pool, iteration)
            pool.wait_ge(s_os, 16 * NB)
            pool.wait_ge(s_x1s, 16 * NB)
            pool.wait_ge(s_qkw, 192 * NB)

        @block.tensor
        def _(pe):
            mmul = nc.tensor.matmul

            class Odd:
                last = {}

                def take(self, i, s, per, off, c, k=BANK_ODD):
                    if k in self.last:
                        s0, per0, off0, c0 = self.last[k]
                        wait(pe, s0, per0, i + off0, c0)
                    self.last[k] = (s, per, off, c)
                    return k

                def next_iteration(self):
                    self.last = {k: (s, per, off - 1, c) for k, (s, per, off, c) in self.last.items()}

            odd = Odd()

            def xpose4(k, src):
                for n in range(4):
                    last = nc.tensor.transpose(ps[:, k, n * P:(n + 1) * P], src(n), ident[:, :])
                return last

            pe.wait_ge(s_cst, N_CST)
            pe.wait_ge(s_wnat, N_WNAT)
            pe.wait_ge(s_set, N_SET)
            for n, m in enumerate((0, 1)):
                xpose4(n, lambda k: x1Toev[:, m, (k % 2) * C + (k // 2) * P:(k % 2) * C + (k // 2) * P + P]).then_inc(s_wT, 1)
            for n in range(2):
                xpose4(2 + n, lambda k: ono[:, 2 * n + k % 2, (k // 2) * P:(k // 2) * P + P]).then_inc(s_wT, 1)
            for n in range(2):
                last = nc.tensor.transpose(ps[:, 4, n * E:(n + 1) * E], vn[0:E, 0, n * P:(n + 1) * P], ident[0:E, 0:E])
            last.then_inc(s_wT, 1)
            pe.wait_ge(s_wev, 5)

            def prepare(i, e):
                if i == 0 or e == 0:
                    n = e + E * i - 1
                    if n >= 0:
                        pe.wait_ge(s_scl, 2 * n + 2)
                        if n >= 2:
                            pe.wait_ge(s_slo, n - 1)
                        xpose4(n % 2, lambda k: rows_gu(n % 2)[:, k % 2, (k // 2) * P:(k // 2) * P + P]).then_inc(s_str, 1)
                        pe.wait_ge(s_drow[n % 2], 16 * (n // 2 + 1))
                        if n >= 1:
                            pe.wait_ge(s_dev, 2 * n)
                        for k in range(2):
                            last = nc.tensor.transpose(ps[:, 2, k * P:(k + 1) * P], rows_dn(n % 2)[:, k, :], ident[:, :])
                        last.then_inc(s_dtr, 1)
                if i == 1 and e == 0:
                    pe.wait_ge(s_dev, 2 * E)
                if i == 1 and e in (2, 3):
                    if e == 2:
                        pe.wait_ge(s_dm, E)
                    else:
                        pe.wait_ge(s_mid, 4)
                    src = (mxd, rwide)[e - 2]
                    for k in range(2):
                        last = nc.tensor.transpose(ps[:, 0, k * P:(k + 1) * P], src[:, k * P:(k + 1) * P], ident[:, :])
                    last.then_inc(s_fin, 1)

            def p1_transpose(i, off, kc, bank=BANK_ODD):
                wait(pe, s_xin, 16, i + off, 16)
                k = odd.take(i, s_xT, 2, off, kc + 1, bank)
                xpose4(k, lambda n: xin[:, n, kc * P:(kc + 1) * P]).then_inc(s_p1t, 1)

            def p1_qk(i, off, n, half, bank=BANK_ODD):
                wait(pe, s_xT, 2, i + off, 2)
                w = (wqT, wkT)[n]
                k = odd.take(i, s_rope, 8, off, 4 * n + 2 * half + 2, bank)
                for kc in range(NC):
                    last = mmul(ps[:, k, :], w[:, kc, half * P:(half + 1) * P], xTden[:, kc, :],
                                start=(kc == 0), stop=(kc == NC - 1))
                last.then_inc(s_p1q, 1)

            def p1_v(i, off, v, bank=BANK_ODD):
                wait(pe, s_xT, 2, i + off, 2)
                k = odd.take(i, s_vx, 2, off, v + 1, bank)
                for m in range(2):
                    t = 2 * v + m
                    for kc in range(NC):
                        last = mmul(ps[:, k, m * C:(m + 1) * C], xTden[:, kc, t * P:(t + 1) * P], wvT[:, kc, :],
                                    start=(kc == 0), stop=(kc == NC - 1))
                last.then_inc(s_p1v, 1)

            def max_unit(i, off, g, m, bank):
                tt, h0, nh = MUNITS[m]
                r, n = g % 2, (tt + 1) * P
                if m == 0:
                    wait(pe, s_stk[r], 2 * 32, i + off, 32 * (g // 2 + 1))
                k = odd.take(i, s_red, NM * NQ, off, NM * g + m + 1, bank)
                for a in range(nh):
                    h = h0 + a
                    mmul(ps[:, k, a * n:(a + 1) * n], qs[0:KS, r, h, tt * P:(tt + 1) * P], ks[0:KS, r, h, 0:n],
                         start=True, stop=False)
                    last = mmul(ps[:, k, a * n + tt * P:(a + 1) * n], identb[:, :], maskq[:, :], start=False, stop=True)
                last.then_inc(s_mx, 1)

            def max_transpose(i, off, g, bank):
                wait(pe, s_spl, 4, i + off, g + 1)
                k = odd.take(i, s_mr, 4, off, g + 1, bank)
                o = ps[:, k, :].bitcast(BF16)
                for t in range(NT):
                    last = nc.tensor.transpose(o[0:12, t * P:(t + 1) * P], mp[:, t, :, :].rearrange("q a h -> q (a h)"), identb[:, :])
                last.then_inc(s_mt, 1)

            def score_step(i, g, k):
                s, p, r = k // 2, k % 2, g % 2
                if k == 0:
                    wait(pe, s_md[r], 32, i, 16 * (g // 2 + 1))
                wait(pe, s_exp, 8 * NQ, i, 8 * g + k)
                n = T - s * P
                for a in range(2):
                    h = 2 * p + a
                    mmul(ps[:, BANK_ST + a, 0:n], ks[0:KX, r, h, s * P:(s + 1) * P], qs[0:KX, r, h, s * P:T],
                         start=True, stop=False)
                    last = mmul(ps[:, BANK_ST + a, 0:P], identb[:, :], maskk[:, :], start=False, stop=True)
                last.then_inc(s_st, 1)

            def pv(i, g, s):
                wait(pe, s_exp, 8 * NQ, i, 8 * g + 2 * s + 2)
                if g == 0 and s == 0:
                    wait(pe, s_vc, 1, i, 1)
                if s == 0:
                    wait(pe, s_yv, NQ, i, g)
                for j in range(4):
                    last = mmul(ps[32 * j:32 * j + 32, BANK_PV, s * P:T], vx[:, s, 4 * g + j, :],
                                pT[:, j, 0:T - s * P],
                                start=(s == 0), stop=(s == NT - 1), tile_position=(0, 32 * j))
                last.then_inc(s_pv, 1)

            def router_transpose(i, off):
                wait(pe, s_cb, CB, i + off, CB)
                k = odd.take(i, s_cT, 1, off, 1)
                o = ps[:, k, :].bitcast(BF16)
                for t in range(NT):
                    last = nc.tensor.transpose(o[0:3 * E, t * P:(t + 1) * P], cp[:, t, :, :].rearrange("q a e -> q (a e)"), identb[:, :])
                last.then_inc(s_ct, 1)

            def sum_transpose(i, off, v):
                wait(pe, s_ye, 2, i + off, 2)
                k = odd.take(i, s_ln2, LN, off, v + 1)
                xpose4(k, lambda n: x1Toev[:, n % 2, (2 * v + n // 2) * P:(2 * v + n // 2 + 1) * P]).then_inc(s_p5t, 1)

            def project(i, off, v):
                wait(pe, s_yn, 2, i + off, 2)
                k = odd.take(i, s_ln1, LN, off, v + 1)
                for m in range(2):
                    t = 2 * v + m
                    for kc in range(NC):
                        last = mmul(ps[:, k, m * C:(m + 1) * C], ynum[:, kc, t * P:(t + 1) * P], wpT[:, kc, :],
                                    start=(kc == 0), stop=(kc == NC - 1))
                last.then_inc(s_prj, 1)

            def x1_transpose(i, off, kc):
                wait(pe, s_x1, NT, i + off, NT)
                k = odd.take(i, s_x1T, 4, off, 2 * kc + 2)
                xpose4(k, lambda n: x1[:, n, kc * P:(kc + 1) * P]).then_inc(s_x1t, 1)

            def router(i, off):
                wait(pe, s_x1T, 4, i + off, 4)
                k = odd.take(i, s_rt, RT, off, 1)
                for t in range(NT):
                    for kc in range(NC):
                        last = mmul(ps[:, k, t * E:(t + 1) * E], x1Toev[:, kc, t * P:(t + 1) * P], gateT[:, kc, :],
                                    start=(kc == 0), stop=(kc == NC - 1))
                last.then_inc(s_gt, 1)

            def hilo(o, w_hi, w_lo, x_hi, x_lo, start, stop):
                n = len(w_hi)
                for k in range(n):
                    mmul(o, w_hi[k], x_hi[k], start=start and k == 0, stop=False)
                    mmul(o, w_lo[k], x_hi[k], start=False, stop=False)
                    last = mmul(o, w_hi[k], x_lo[k], start=False, stop=stop and k == n - 1)
                return last

            def gate_or_up(b, e, m, apart):
                bank, used, done = ((BANK_G, s_t1 if apart else s_t3, s_g), (BANK_U, s_t2, s_u))[m]
                if e == 0 and m == 0:
                    wait(pe, s_ch, 1, b, 1)
                    wait(pe, s_cur, 2, b, 1)
                wait(pe, used, E, b, e)
                hilo(ps[:, bank, :], [gu_hi[:, e, kc, m, :] for kc in range(NC)],
                     [gu_lo[:, e, kc, m, :] for kc in range(NC)],
                     [xh[:, kc, :] for kc in range(NC)], [xl[:, kc, :] for kc in range(NC)],
                     True, True).then_inc(done, 1)

            def weights_out(b, e, bank):
                wait(pe, s_t1, E, b, e + 1)
                if e == 0:
                    wait(pe, s_cur, 2, b, 2)
                if bank != BANK_G:
                    wait(pe, s_t3, E, b, e)
                mmul(ps[:, bank, :], selT[:, e:e + 1].to_broadcast([3 * E, P]), combT[:, :],
                     start=True, stop=True).then_inc(s_bc, 1)

            def down(b, e, m):
                if e == 0 and m == 0:
                    wait(pe, s_ye, 2, b, 0)
                if m == 0:
                    wait(pe, s_h, E, b, e + 1)
                r = e % 2
                last = hilo(ps[:, BANK_Y + m, :], [dn[:, e, 0, m * P:(m + 1) * P]],
                            [dn[:, e, 1, m * P:(m + 1) * P]], [hh[:, r, :]], [hl[:, r, :]], e == 0, e == E - 1)
                if m == NC - 1:
                    last.then_inc(s_d, 1)

            def odd_job(i, e, place):
                last_ln, end, nxt = has(i, 3, NB + 2), has(i, 1, NB), has(i, 0, NB - 2)
                if place == 1:
                    if e in SLOT_SUM and last_ln:
                        sum_transpose(i, -3, SLOT_SUM.index(e))
                    if e in SLOT_PROJECT and end:
                        project(i, -1, SLOT_PROJECT.index(e))
                    if e in SLOT_X and nxt:
                        p1_transpose(i, 1, SLOT_X.index(e))
                    if e in SLOT_X1 and end:
                        x1_transpose(i, -1, SLOT_X1.index(e))
                    if e in SLOT_Q and nxt:
                        p1_qk(i, 1, 0, SLOT_Q.index(e))
                    if e == SLOT_ROUTER and end:
                        router(i, -1)
                    if e in SLOT_V and nxt:
                        p1_v(i, 1, SLOT_V.index(e))
                    if e in SLOT_K and nxt:
                        p1_qk(i, 1, 1, SLOT_K.index(e))
                    if e == SLOT_WEIGHTS and end:
                        router_transpose(i, -1)
                g, le = e // LE, e % LE
                if has(i, 0, NB - 1) if g < NQ - 1 else nxt:
                    off, q = (0, g + 1) if g < NQ - 1 else (1, 0)
                    slots, _, turn = max_slots(i)
                    if (le, place) in slots:
                        max_unit(i, off, q, slots[le, place], max_bank(i, place))
                    if (le, place) == turn:
                        max_transpose(i, off, q, max_bank(i, place))

            def iteration(i):
                experts, attention, b = has(i, 2, NB + 1), has(i, 0, NB - 1), i - 2
                if isinstance(i, int) and i == 2:
                    pe.wait_ge(s_dlo, E // 2)
                    pe.wait_ge(s_slo, E)
                apart = not has(i, 0, NB - 1)
                for e in range(E):
                    g, le = e // LE, e % LE
                    if experts:
                        gate_or_up(b, e, 0, apart and e > 0)
                    if attention:
                        score_step(i, g, le)
                    odd_job(i, e, 0)
                    if experts:
                        gate_or_up(b, e, 1, apart)
                    odd_job(i, e, 1)
                    late = has(i, 3, NB + 2) if e < 2 else experts
                    of, d = (b - 1, e - 2 + E) if e < 2 else (b, e - 2)
                    if late and apart:
                        for m in range(NC):
                            down(of, d, m)
                    if experts:
                        weights_out(b, e, BANK_ST if apart else BANK_G)
                    if late and not apart:
                        for m in range(NC):
                            down(of, d, m)
                    odd_job(i, e, 2)
                    if attention and le % 2:
                        pv(i, g, le // 2)
                    if isinstance(i, int) and i < 2:
                        prepare(i, e)
                odd.next_iteration()

            for kc in range(NC):
                p1_transpose(0, 0, kc, FIRST_X[kc])
            for n in range(2):
                for half in range(2):
                    p1_qk(0, 0, n, half, FIRST_QK[n][half])
            for v in range(2):
                p1_v(0, 0, v, FIRST_V[v])
            for m in range(NM):
                max_unit(0, 0, 0, m, max_bank(0, m % 2))
            max_transpose(0, 0, 0, max_bank(0, 0))
            iterations(pe, iteration)

        @block.scalar
        def _(act):
            def actv(o, i, f, **k):
                return nc.scalar.activation(o, i, f, **k)

            act.wait_ge(s_set, N_SET)
            for n, dst in enumerate((wqT, wkT, wvT, wpT)):
                act.wait_ge(s_wT, n + 1)
                actv(dst[:, :, :].rearrange("p a b -> p (a b)"), ps[:, n, :], ACT.Copy).then_inc(s_wev, 1)
            act.wait_ge(s_wT, 5)
            actv(gateT[:, :, :].rearrange("p a b -> p (a b)"), ps[:, 4, 0:2 * E], ACT.Copy).then_inc(s_wev, 1)

            def scale_rows(i, e):
                n = e + E * i - 1
                if 0 <= n < E:
                    act.wait_ge(s_sv, 3 * n + 3)
                    for m in range(2):
                        actv(rows_gu(n % 2)[:, m, :], rows_gu(n % 2)[:, m, :], ACT.Copy,
                             scale=rcp[:, n % 2, m:m + 1]).then_inc(s_scl, 1)

            def prepare(i, e):
                if i == 0 or e == 0:
                    n = e + E * i - 1
                    if n >= 0:
                        act.wait_ge(s_str, n + 1)
                        if n >= 2:
                            act.wait_ge(s_slo, n - 1)
                        actv(gu_hi[:, n].rearrange("p a b f -> p (a b f)"), ps[:, n % 2, :], ACT.Copy).then_inc(s_shi, 1)
                        act.wait_ge(s_dtr, n + 1)
                        act.wait_ge(s_mm, n + 1)
                        actv(products(n, 1)[:, 0, :], ps[:, 2, 0:C], ACT.Copy, scale=mm[:, n:n + 1]).then_inc(s_dev, 1)
                        if n >= 2:
                            act.wait_ge(s_dm, n - 1)
                        actv(sizes(n % 2), ps[:, 2, 0:C], ACT.Abs, scale=mm[:, n:n + 1]).then_inc(s_dev, 1)
                        if n + 2 < E:
                            load_rows(act, n + 2)
                if i == 1 and e == 3:
                    act.wait_ge(s_fin, 2)
                    actv(rinvb, ps[:, 0, 0:C], ACT.Copy).then_inc(s_rb, 1)
                n = e - 5
                if i == 1 and 0 <= n < E // 2:
                    act.wait_ge(s_dsc, n + 1)
                    actv(dn[:, 2 * n:2 * n + 2, 0, :], scaled(n % 2), ACT.Copy).then_inc(s_dhi, 1)

            def x_out(b, kc, bank=BANK_ODD):
                wait(act, s_yn, 2, b, -2)
                wait(act, s_p1v, 2, b, 0)
                wait(act, s_p1q, 4, b, 0)
                wait(act, s_p1t, 2, b, kc + 1)
                actv(xTden[:, kc, :], ps[:, bank, :], ACT.Copy).then_inc(s_xT, 1)

            def x1_out(i, kc):
                wait(act, s_ch, 1, i, 0)
                wait(act, s_gt, 1, i, 0)
                wait(act, s_xl, 1, i, 0)
                wait(act, s_p5t, 2, i - 2, 2)
                wait(act, s_x1t, 2, i, kc + 1)
                actv(x1Toev[:, kc, :], ps[:, BANK_ODD, :], ACT.Copy).then_inc(s_x1T, 1)
                actv(xh_n[:, kc, :], ps[:, BANK_ODD, :], ACT.Copy).then_inc(s_x1T, 1)

            def sum_out(b):
                wait(act, s_d, E, b, E)
                if isinstance(b, int):
                    wait(act, s_p5t, 2, b, 0)
                if not (isinstance(b, int) and b + 1 > NB - 1):
                    wait(act, s_gt, 1, b, 2)
                    wait(act, s_xl, 1, b, 2)
                for m in range(NC):
                    actv(x1Toev[:, m, :], ps[:, BANK_Y + m, :], ACT.Copy, scale=rc[:, m:m + 1]).then_inc(s_ye, 1)

            def tokens_in(b):
                wait(act, s_u, E, b, 0)
                wait(act, s_x1T, 4, b, 4)
                actv(xh[:, :, :], xh_n[:, :, :], ACT.Copy).then_inc(s_ch, 1)

            def router_exp(b):
                wait(act, s_rt, RT, b, RT)
                wait(act, s_cb, CB, b, 0)
                actv(le[:, :, :], lg[:, :, :], ACT.Exp).then_inc(s_le, 1)

            def router_out(b):
                wait(act, s_ct, 1, b, 1)
                wait(act, s_cur, 2, b, 0)
                actv(combT_n[:, :], ps[0:3 * E, BANK_ODD, :].bitcast(BF16)[:, 0:T], ACT.Copy).then_inc(s_cT, 1)

            def max_out(b, g, bank):
                wait(act, s_mt, 4, b, g + 1)
                wait(act, s_md[(g + 1) % 2], 32, b, 16 * ((g + 1) // 2))
                actv(mrow[:, :], ps[0:12, bank, :].bitcast(BF16)[:, 0:T], ACT.Copy).then_inc(s_mr, 1)

            def exp_step(i, g, k):
                s, p = k // 2, k % 2
                n = T - s * P
                wait(act, s_st, 8 * NQ, i, 8 * g + k + 1)
                wait(act, s_pv, 4 * NQ, i, 4 * g + s)
                actv(pT[:, 2 * p:2 * p + 2, 0:n], ps[:, BANK_ST:BANK_ST + 2, 0:n], ACT.Exp,
                     scale=float(1.0 / np.sqrt(np.float32(D)))).then_inc(s_exp, 1)

            def attention_out(i, g):
                r = g % 2
                wait(act, s_pv, 4 * NQ, i, 4 * g + 4)
                wait(act, s_yw[r], 32, i, 16 * (g // 2))
                actv(yev[:, r, :], ps[:, BANK_PV, :], ACT.Copy).then_inc(s_yv, 1)
                wait(act, s_yv, NQ, i, g + 1)
                dst = att_dram[i, 4 * g:4 * g + 4] if isinstance(i, int) else \
                    att_dram[bass.ds(i, 1), 4 * g:4 * g + 4].rearrange("o h w d t -> (o h) w d t")
                act.dma_start(dst.rearrange("h w d t -> (h w d) t"), yev[:, r, :]).then_inc(s_yw[r], 16)

            def tanh(b, e):
                wait(act, s_g, E, b, e + 1)
                wait(act, s_h, E, b, e - 1)
                actv(hf[:, e % 2, :], ps[:, BANK_G, :], ACT.Tanh, scale=mgh[:, e:e + 1]).then_inc(s_th, 1)

            def upper(b, e):
                wait(act, s_t3, E, b, e + 1)
                wait(act, s_d, E, b, e - 1)
                actv(hh[:, e % 2, :], hf[:, e % 2, :], ACT.Copy).then_inc(s_hh, 1)

            def iteration(i):
                experts, attention, b = has(i, 2, NB + 1), has(i, 0, NB - 1), i - 2
                end, nxt = has(i, 1, NB), has(i, 0, NB - 2)
                if isinstance(i, int) and i == 2:
                    act.wait_ge(s_dlo, E // 2)
                for e in range(E):
                    g, le = e // LE, e % LE
                    if experts:
                        tanh(b, e)
                        if e > 0:
                            upper(b, e - 1)
                    if e == 0 and end:
                        attention_out(i - 1, NQ - 1)
                    if attention:
                        if le == 0 and g > 0:
                            attention_out(i, g - 1)
                        exp_step(i, g, le)
                    if isinstance(i, int) and i < 2:
                        scale_rows(i, e)
                    if e == 1 and has(i, 3, NB + 2):
                        sum_out(i - 3)
                    turn = max_slots(i)[2]
                    if le == turn[0] and (attention if g < NQ - 1 else nxt):
                        if g < NQ - 1:
                            max_out(i, g + 1, max_bank(i, turn[1]))
                        else:
                            max_out(i + 1, 0, max_bank(i, turn[1]))
                    if e in SLOT_X and nxt:
                        x_out(i + 1, SLOT_X.index(e))
                    if e in SLOT_X1 and end:
                        x1_out(i - 1, SLOT_X1.index(e))
                    if e == SLOT_ROUTER + 3 and end:
                        router_exp(i - 1)
                    if e == SLOT_WEIGHTS and end:
                        router_out(i - 1)
                    if isinstance(i, int) and i < 2:
                        prepare(i, e)
                if end:
                    tokens_in(i - 1)
                if experts:
                    upper(b, E - 1)
            for kc in range(NC):
                x_out(0, kc, FIRST_X[kc])
            max_out(0, 0, max_bank(0, 0))
            iterations(act, iteration)

        @block.vector
        def _(dve):
            V = nc.vector

            dve.wait_ge(s_cst, N_CST)
            V.tensor_copy(identb[:, :], ident[:, :]).then_inc(s_set, 1)
            V.tensor_copy(maskq[:, :], x1[:, 0, 0:P]).then_inc(s_set, 1)
            V.tensor_copy(maskk[:, :], x1[:, 1, 0:P]).then_inc(s_set, 1)
            for n in range(3):
                V.tensor_copy(selT[E * n:E * n + E, :], ident[E * n:E * n + E, E * n:E * n + E]).then_inc(s_set, 1)
            V.memset(ks[KS:KX, :, :, :], 1.0).then_inc(s_set, 1)
            V.memset(vx[:, :, :, D:2 * D], 1.0).then_inc(s_set, 1)
            V.memset(mhalf[:, :], -0.5).then_inc(s_set, 1)
            dve.wait_ge(s_set, N_SET)

            def prepare(i, e):
                if i == 0:
                    r = e % 2
                    dve.wait_ge(s_row[r], 16 * (e // 2 + 1))
                    V.tensor_reduce(mx2[:, r, :], rows_gu(r), axis=AX.X, op=ALU.max,
                                    apply_absolute_value=True).then_inc(s_sv, 1)
                    dve.wait_ge(s_sv, 3 * e + 1)
                    V.tensor_scalar_max(mgu[:, e, :], mx2[:, r, :], 1e-15).then_inc(s_sv, 1)
                    dve.wait_ge(s_sv, 3 * e + 2)
                    if e >= 2:
                        dve.wait_ge(s_scl, 2 * e - 2)
                    V.reciprocal(rcp[:, r, :], mgu[:, e, :]).then_inc(s_sv, 1)
                    if e == 0:
                        dve.wait_ge(s_wT, 4)
                    V.scalar_tensor_tensor(out=mm[:, e:e + 1], in0=mgu[:, e, 0:1], scalar=4.0, in1=mgu[:, e, 1:2],
                                           op0=ALU.mult, op1=ALU.mult).then_inc(s_mm, 1)
                if i == 0 or e < 2:
                    n = e + E * i - 2
                    if n >= 0:
                        dve.wait_ge(s_shi, n + 1)
                        V.tensor_tensor(gu_lo[:, n].rearrange("p a b f -> p (a b f)"), ps[:, n % 2, :],
                                        gu_hi[:, n].rearrange("p a b f -> p (a b f)"), ALU.subtract).then_inc(s_slo, 1)
                        dve.wait_ge(s_dev, 2 * n + 2)
                        if n > 0:
                            dve.wait_ge(s_dm, n)
                        V.tensor_tensor(mxd, sizes(n % 2), mxd if n else sizes(0), ALU.max).then_inc(s_dm, 1)
                if i == 1 and e == 2:
                    dve.wait_ge(s_fin, 1)
                    V.tensor_reduce(rinv[:, :], ps[:, 0, 0:C].rearrange("p (m f) -> p m f", m=NC), axis=AX.X,
                                    op=ALU.max).then_inc(s_mid, 1)
                    dve.wait_ge(s_mid, 1)
                    V.tensor_scalar_max(rc[:, :], rinv[:, :], 1e-30).then_inc(s_mid, 1)
                    dve.wait_ge(s_mid, 2)
                    V.reciprocal(rinv[:, :], rc[:, :]).then_inc(s_mid, 1)
                    dve.wait_ge(s_mid, 3)
                    V.tensor_copy(rwide.rearrange("p (m f) -> p m f", m=NC), along(rinv[:, :], P)).then_inc(s_mid, 1)
                    V.tensor_scalar(mgh[:, :], mgu[:, :, 0], 0.5, None, ALU.mult).then_inc(s_mid, 1)
                n = e - 4
                if i == 1 and 0 <= n < E // 2:
                    dve.wait_ge(s_rb, 1)
                    if n >= 2:
                        dve.wait_ge(s_dlo, n - 1)
                    V.tensor_tensor(scaled(n % 2), products(2 * n, 2), under(rinvb, 2), ALU.mult).then_inc(s_dsc, 1)
                n = e - 5
                if i == 1 and 0 <= n < E // 2:
                    dve.wait_ge(s_dhi, n + 1)
                    V.tensor_tensor(dn[:, 2 * n:2 * n + 2, 1, :], scaled(n % 2), dn[:, 2 * n:2 * n + 2, 0, :],
                                    ALU.subtract).then_inc(s_dlo, 1)

            def rope(b, n, half, bank=BANK_ODD):
                wait(dve, s_pp, 2, b, n)
                if n == 0:
                    wait(dve, s_prj, 2, b, -2)
                bias = (bqc, bkc)[n]
                wait(dve, s_p1q, 4, b, 2 * n + half + 1)
                for dst, tab in ((qf[:, half, :], cosT), (ynum[:, 1 - half, :], sinT)):
                    V.scalar_tensor_tensor(out=dst, in0=ps[:, bank, :], scalar=bias[:, half:half + 1], in1=tab[:, :],
                                           op0=ALU.add, op1=ALU.mult).then_inc(s_rope, 1)

            def values(b, v, bank=BANK_ODD):
                wait(dve, s_vc, 1, b, 0)
                wait(dve, s_p1v, 2, b, v + 1)
                V.tensor_tensor(vn[:, 2 * v:2 * v + 2, :],
                                ps[:, bank, :].rearrange("p (m c) -> p m c", m=2),
                                under(bv_b[:, :], 2), ALU.add).then_inc(s_vx, 1)

            def reduce_unit(b, g, m, bank):
                tt, h0, nh = MUNITS[m]
                n = (tt + 1) * P
                wait(dve, s_mx, NM * NQ, b, NM * g + m + 1)
                V.tensor_reduce(mn[:, tt, h0:h0 + nh],
                                ps[:, bank, 0:nh * n].rearrange("p (a n) -> p a n", a=nh),
                                axis=AX.X, op=ALU.max, negate=True).then_inc(s_red, 1)

            def split_max(b, g):
                wait(dve, s_red, NM * NQ, b, NM * g + NM)
                wait(dve, s_mt, 4, b, g)
                V.tensor_copy(mp[:, :, 0, :], mn[:, :, :]).then_inc(s_spl2, 1)
                wait(dve, s_spl2, 12, b, 3 * g + 1)
                V.tensor_tensor(mr[:, :, :], mn[:, :, :], mp[:, :, 0, :], ALU.subtract).then_inc(s_spl2, 1)
                wait(dve, s_spl2, 12, b, 3 * g + 2)
                V.tensor_copy(mp[:, :, 1, :], mr[:, :, :]).then_inc(s_spl2, 1)
                wait(dve, s_spl2, 12, b, 3 * g + 3)
                V.tensor_tensor(mp[:, :, 2, :], mr[:, :, :], mp[:, :, 1, :], ALU.subtract).then_inc(s_spl, 1)

            def router_weights(b, part):
                n = [4 * part]

                def step(ins):
                    n[0] += 1
                    ins.then_inc(s_cb, 1)
                    wait(dve, s_cb, CB, b, n[0])
                if part == 0:
                    wait(dve, s_le, 1, b, 1)
                    wait(dve, s_ct, 1, b, 0)
                    step(V.tensor_tensor(le[:, :, :], le[:, :, :], msk[:, :, :], ALU.mult))
                    step(V.tensor_reduce(sm[:, :], le[:, :, :], axis=AX.X, op=ALU.add))
                    step(V.reciprocal(sm[:, :], sm[:, :]))
                    step(V.tensor_tensor(le[:, :, :], le[:, :, :], along(sm[:, :], E), ALU.mult))
                else:
                    step(V.tensor_copy(cp[:, :, 0, :], le[:, :, :]))
                    step(V.tensor_tensor(le[:, :, :], le[:, :, :], cp[:, :, 0, :], ALU.subtract))
                    step(V.tensor_copy(cp[:, :, 1, :], le[:, :, :]))
                    step(V.tensor_tensor(cp[:, :, 2, :], le[:, :, :], cp[:, :, 1, :], ALU.subtract))

            def router_in(i):
                wait(dve, s_gt, 1, i, 1)
                V.tensor_copy(lg[:, :, :], ps[:, BANK_ODD, 0:NT * E].rearrange("p (t e) -> p t e", t=NT)).then_inc(s_rt, 1)

            def router_choice(i, part):
                if part == 0:
                    wait_apart(dve, s_rt, i * RT + 1)
                    for t in range(NT):
                        V.max(v8[:, t, :], lg[:, t, :]).then_inc(s_rt, 1)
                    return
                wait_apart(dve, s_rt, i * RT + 1 + NT)
                for t in range(NT):
                    V.match_replace(lg2[:, t, :], v8[:, t, :], lg[:, t, :], -3.0e38).then_inc(s_rt, 1)
                wait(dve, s_rt, RT, i, 1 + 2 * NT)
                V.tensor_tensor(msk[:, :, :], lg2[:, :, :], lg[:, :, :], ALU.not_equal).then_inc(s_rt, 1)
                V.tensor_tensor(lg[:, :, :], lg[:, :, :], along(v8[:, :, 0], E), ALU.subtract).then_inc(s_rt, 1)

            def ln_add(which, b, v):
                s, dst, done = ((s_ln1, x1, s_prj), (s_ln2, ono, s_p5t))[which]
                wait(dve, done, 2, b, v + 1)
                if v == 0:
                    wait(dve, (s_xb, s_xo)[which], (1, 16)[which], b, (1, 16)[which])
                part = dst[:, 2 * v:2 * v + 2, :].rearrange("p n c -> p (n c)")
                V.tensor_tensor(part, part, ps[:, BANK_ODD, :], ALU.add).then_inc(s, 1)

            def ln_stats(which, b, v):
                s, dst = ((s_ln1, x1), (s_ln2, ono))[which]
                tiles = range(2 * v, 2 * v + 2)
                wait(dve, s, LN, b, 2)
                for t in tiles:
                    V.bn_stats(st[:, which, t, :], dst[:, t, :]).then_inc(s, 1)
                wait_apart(dve, s, b * LN + 4 * v + 4)
                for t in tiles:
                    V.bn_aggr(mv[:, which, t, :], st[:, which, t, :]).then_inc(s, 1)

            def gated(b, e):
                wait(dve, s_th, E, b, e + 1)
                h = hf[:, e % 2, :]
                V.scalar_tensor_tensor(out=h, in0=h, scalar=1.0, in1=ps[:, BANK_G, :],
                                       op0=ALU.add, op1=ALU.mult).then_inc(s_t1, 1)

            def times_up(b, e):
                wait(dve, s_u, E, b, e + 1)
                wait(dve, s_t1, E, b, e + 1)
                h = hf[:, e % 2, :]
                V.scalar_tensor_tensor(out=h, in0=h, scalar=0.125, in1=ps[:, BANK_U, :],
                                       op0=ALU.mult, op1=ALU.mult).then_inc(s_t2, 1)

            def times_weight(b, e, bank):
                wait(dve, s_bc, E, b, e + 1)
                wait(dve, s_t2, E, b, e + 1)
                h = hf[:, e % 2, :]
                V.tensor_tensor(h, h, ps[:, bank, :], ALU.mult).then_inc(s_t3, 1)

            def lower(b, e):
                wait(dve, s_hh, E, b, e + 1)
                wait(dve, s_d, E, b, e - 1)
                V.tensor_tensor(hl[:, e % 2, :], hf[:, e % 2, :], hh[:, e % 2, :], ALU.subtract).then_inc(s_h, 1)

            def tokens_in(b):
                wait(dve, s_u, E, b, 0)
                wait(dve, s_xl, 1, b, 1)
                V.tensor_copy(xl[:, :, :], xl_n[:, :, :]).then_inc(s_cur, 1)

            def weights_in(b):
                wait(dve, s_bc, E, b, 0)
                wait(dve, s_cT, 1, b, 1)
                V.tensor_copy(combT[:, :], combT_n[:, :]).then_inc(s_cur, 1)

            def last_norm(b):
                dve.wait_ge(s_rs2, b + 1)
                for t in range(NT):
                    V.tensor_scalar(ono[:, t, :], ono[:, t, :], mv[:, 1, t, 0:1], rs[:, 1, t:t + 1],
                                    ALU.subtract, ALU.mult).then_inc(s_o, 1)

            def reciprocals(b):
                wait(dve, s_dn, 16, b, 16)
                V.reciprocal(den[:, :], den[:, :]).then_inc(s_yr, 1)

            def divide(b, c):
                wait(dve, s_yd, 64, b, 64)
                V.tensor_tensor(ynum[:, c, :], ynum[:, c, :], xTden[:, c, :], ALU.mult).then_inc(s_yn, 1)

            def odd_job(i, e, place):
                last_ln, end, nxt = has(i, 3, NB + 2), has(i, 1, NB), has(i, 0, NB - 2)
                if place == 1:
                    if e in SLOT_SUM and last_ln:
                        ln_add(1, i - 3, SLOT_SUM.index(e))
                    if e in SLOT_PROJECT and end:
                        ln_add(0, i - 1, SLOT_PROJECT.index(e))
                    if e in SLOT_Q and nxt:
                        rope(i + 1, 0, SLOT_Q.index(e))
                    if e == SLOT_ROUTER and end:
                        router_in(i - 1)
                    if e in SLOT_V and nxt:
                        values(i + 1, SLOT_V.index(e))
                    if e in SLOT_K and nxt:
                        rope(i + 1, 1, SLOT_K.index(e))
                g, le = e // LE, e % LE
                slots, split, _ = max_slots(i)
                if (le, place) in slots:
                    if g < NQ - 1 and has(i, 0, NB - 1):
                        reduce_unit(i, g + 1, slots[le, place], max_bank(i, place))
                    if g == NQ - 1 and nxt:
                        reduce_unit(i + 1, 0, slots[le, place], max_bank(i, place))
                if (le, place) == split:
                    if g < NQ - 1 and has(i, 0, NB - 1):
                        split_max(i, g + 1)
                    if g == NQ - 1 and nxt:
                        split_max(i + 1, 0)

            def iteration(i):
                experts, b = has(i, 2, NB + 1), i - 2
                last_ln, end = has(i, 3, NB + 2), has(i, 1, NB)
                if last_ln:
                    lower(i - 3, E - 1)
                for e in range(E):
                    le = e % LE
                    first = le == 3 or e in ODD_SLOTS
                    if first:
                        odd_job(i, e, 0)
                    if experts:
                        gated(b, e)
                    if not first:
                        odd_job(i, e, 0)
                    if experts:
                        times_up(b, e)
                    first = 0 < le < LE - 1
                    if first:
                        odd_job(i, e, 1)
                    if e == E - 1 and end:
                        tokens_in(i - 1)
                    if experts:
                        times_weight(b, e, BANK_G if has(i, 0, NB - 1) else BANK_ST)
                        if e > 0:
                            lower(b, e - 1)
                    if not first:
                        odd_job(i, e, 1)
                    if e == E - 1 and end:
                        weights_in(i - 1)
                    odd_job(i, e, 2)
                    if e == 2 and end:
                        reciprocals(i - 1)
                    if e == 4 and end:
                        for c in range(NC):
                            divide(i - 1, c)
                    if e in SLOT_STATS[0] and end:
                        ln_stats(0, i - 1, SLOT_STATS[0].index(e))
                    if e in SLOT_STATS[1] and last_ln:
                        ln_stats(1, i - 3, SLOT_STATS[1].index(e))
                    if e == SLOT_STATS[1][1] and isinstance(i, int) and i == NB + 2:
                        last_norm(i - 3)
                    if e in (SLOT_ROUTER, SLOT_ROUTER + 1) and end:
                        router_choice(i - 1, e - SLOT_ROUTER)
                    if e in (SLOT_WEIGHTS - 3, SLOT_WEIGHTS - 2) and end:
                        router_weights(i - 1, e - (SLOT_WEIGHTS - 3))
                    if isinstance(i, int) and i < 2:
                        prepare(i, e)

            def split_first(n):
                dve.wait_ge(s_rope, 4 * n + 4)
                V.tensor_tensor(qf[:, 0, :], qf[:, 0, :], ynum[:, 0, :], ALU.subtract).then_inc(s_pp2, 1)
                V.tensor_tensor(qf[:, 1, :], qf[:, 1, :], ynum[:, 1, :], ALU.add).then_inc(s_pp2, 1)
                if n == 1:
                    dve.wait_ge(s_qkw, 96)
                for part in range(2):
                    dve.wait_ge(s_pp2, 5 * n + 2 + 2 * part)
                    V.tensor_copy(pbuf[:, :, part, :], qf[:, :, :]).then_inc(s_pp2, 1)
                    dve.wait_ge(s_pp2, 5 * n + 3 + 2 * part)
                    if part == 0:
                        V.tensor_tensor(qf[:, :, :], qf[:, :, :], pbuf[:, :, 0, :], ALU.subtract).then_inc(s_pp2, 1)
                    else:
                        V.tensor_tensor(pbuf[:, :, 2, :], qf[:, :, :], pbuf[:, :, 1, :], ALU.subtract).then_inc(s_pp, 1)

            for n in range(2):
                for half in range(2):
                    rope(0, n, half, FIRST_QK[n][half])
                split_first(n)
            for v in range(2):
                values(0, v, FIRST_V[v])
            for m in range(NM):
                reduce_unit(0, 0, m, max_bank(0, m % 2))
            split_max(0, 0)
            iterations(dve, iteration)


def tables():
    i = np.arange(HALF, dtype=np.float32)
    alpha = (np.float32(1.0) / np.power(np.float32(10000.0), np.float32(2.0) * i / np.float32(D))).astype(np.float32)
    ang = np.arange(T, dtype=np.float32)[:, None] * alpha
    rows = np.tile(ang.T, (H, 1))
    cos_t, sin_t = np.cos(rows).astype(np.float32), np.sin(rows).astype(np.float32)
    r = np.arange(P)
    above = np.where(r[None, :] > r[:, None], np.float32(NEG), np.float32(0))
    return {"cos_t": cos_t, "sin_t": sin_t, "ident_h": np.eye(P, dtype=np.float32),
            "mask_h": np.ascontiguousarray(np.stack([above, above.T]))}


_INS = ["L0_attn_x", "L0_attn_wq", "L0_attn_bq", "L0_attn_wk", "L0_attn_bk", "L0_attn_wv", "L0_attn_bv",
        "L0_attn_wp", "L0_attn_bp", "L0_ffn_gate_w", "L0_ffn_gate_up_w", "L0_ffn_down_w"]


def kernel(**inputs):
    import concourse.bacc as _bacc
    from concourse.bass_utils import run_bass_kernel_spmd as _run

    nc = _bacc.Bacc("TRN2", target_bir_lowering=False, num_devices=1)
    arrays = {name: np.ascontiguousarray(inputs[name]) for name in _INS}
    arrays.update(tables())
    args = [nc.dram_tensor(name, a.shape, mybir.dt.from_np(a.dtype), kind="ExternalInput").ap()
            for name, a in arrays.items()]
    out = nc.dram_tensor("out", (B, T, C), F32, kind="ExternalOutput").ap()
    build(nc, *args, out)
    return _run(nc, [arrays], core_ids=[0]).results[0]["out"]
```
